# Optimizing a Trainium2 kernel written in Bass

```python
import numpy as np
import jax
import jax.numpy as jnp

def _softmax(x, axis=-1):
    return jax.nn.softmax(x, axis=axis)

def _gelu(x):
    return jax.nn.gelu(x, approximate=True)

def _silu(x):
    return jax.nn.silu(x)

def _sigmoid(x):
    return jax.nn.sigmoid(x)

def _layernorm(x, axis=-1, eps=1e-05):
    m = jnp.mean(x, axis=axis, keepdims=True)
    v = jnp.var(x, axis=axis, keepdims=True)
    return (x - m) / jnp.sqrt(v + eps)

def _scatter_add(tgt, idx, src, axis=0):
    return tgt.at[idx].add(src)

def _segment_sum(src, seg, n):
    return jax.ops.segment_sum(src, seg, n)
kernel_name = 'mk_prb_d1_jaxref_r8_240170'

def setup_inputs(seed: int=0):
    np.random.seed(seed)
    _w = jnp.asarray

    def _L0_attn_setup():
        import jax, jax.numpy as jnp
        import numpy as np
        DIM = 128
        HEADS = 16
        HEAD_DIM = DIM // HEADS
        B, S = (4, 512)
        key = jax.random.key(seed)
        ks = jax.random.split(key, 8)
        sc = 1.0 / np.sqrt(DIM)
        return {'x': jax.random.normal(ks[0], (B, S, DIM), dtype=jnp.float32), 'Wq': jax.random.normal(ks[1], (DIM, DIM), dtype=jnp.float32) * sc, 'Wk': jax.random.normal(ks[2], (DIM, DIM), dtype=jnp.float32) * sc, 'Wv': jax.random.normal(ks[3], (DIM, DIM), dtype=jnp.float32) * sc, 'Wp': jax.random.normal(ks[4], (DIM, DIM), dtype=jnp.float32) * sc, 'bp': jnp.zeros((DIM,), dtype=jnp.float32), 'conv_w': jax.random.normal(ks[5], (DIM, 3), dtype=jnp.float32) * (1.0 / np.sqrt(3.0)), 'conv_b': jnp.zeros((DIM,), dtype=jnp.float32)}
    _L0_attn_in = _L0_attn_setup()

    def _L0_ffn_setup():
        import jax, jax.numpy as jnp
        import numpy as np
        B, S, D = (4, 256, 128)
        F = 344
        E = 8
        TOPK = 2

        def _ffn(x, gw, uw, dw):
            return jax.nn.silu(x @ gw) * (x @ uw) @ dw
        key = jax.random.key(seed)
        ks = jax.random.split(key, 10)
        sc = 0.02
        return {'x': jax.random.normal(ks[0], (B, S, D), dtype=jnp.float32), 'router_w': jax.random.normal(ks[1], (D, E), dtype=jnp.float32) * sc, 'router_b': jnp.zeros((E,), dtype=jnp.float32), 'gate_w': jax.random.normal(ks[2], (E, D, F), dtype=jnp.float32) * sc, 'up_w': jax.random.normal(ks[3], (E, D, F), dtype=jnp.float32) * sc, 'down_w': jax.random.normal(ks[4], (E, F, D), dtype=jnp.float32) * sc, 'sh_gate_w': jax.random.normal(ks[5], (D, F), dtype=jnp.float32) * sc, 'sh_up_w': jax.random.normal(ks[6], (D, F), dtype=jnp.float32) * sc, 'sh_down_w': jax.random.normal(ks[7], (F, D), dtype=jnp.float32) * sc}
    _L0_ffn_in = _L0_ffn_setup()
    _d = {'L0_attn_x': _L0_attn_in['x'], 'L0_attn_Wq': _L0_attn_in['Wq'], 'L0_attn_Wk': _L0_attn_in['Wk'], 'L0_attn_Wv': _L0_attn_in['Wv'], 'L0_attn_Wp': _L0_attn_in['Wp'], 'L0_attn_bp': _L0_attn_in['bp'], 'L0_attn_conv_w': _L0_attn_in['conv_w'], 'L0_attn_conv_b': _L0_attn_in['conv_b'], 'L0_ffn_router_w': _L0_ffn_in['router_w'], 'L0_ffn_router_b': _L0_ffn_in['router_b'], 'L0_ffn_gate_w': _L0_ffn_in['gate_w'], 'L0_ffn_up_w': _L0_ffn_in['up_w'], 'L0_ffn_down_w': _L0_ffn_in['down_w'], 'L0_ffn_sh_gate_w': _L0_ffn_in['sh_gate_w'], 'L0_ffn_sh_up_w': _L0_ffn_in['sh_up_w'], 'L0_ffn_sh_down_w': _L0_ffn_in['sh_down_w']}
    _x0 = _d['L0_attn_x']
    _d['L0_attn_x'] = jax.random.normal(jax.random.fold_in(jax.random.key(seed), 1), (16, 256, 128), dtype=_x0.dtype)
    del _x0
    return _d

def reference(L0_attn_x, L0_attn_Wq, L0_attn_Wk, L0_attn_Wv, L0_attn_Wp, L0_attn_bp, L0_attn_conv_w, L0_attn_conv_b, L0_ffn_router_w, L0_ffn_router_b, L0_ffn_gate_w, L0_ffn_up_w, L0_ffn_down_w, L0_ffn_sh_gate_w, L0_ffn_sh_up_w, L0_ffn_sh_down_w):

    def _L0_attn_ref(x, Wq, Wk, Wv, Wp, bp, conv_w, conv_b):
        import jax, jax.numpy as jnp
        import numpy as np
        DIM = 128
        HEADS = 16
        HEAD_DIM = DIM // HEADS
        B, S = (4, 512)
        b, s, d = x.shape

        def split_heads(t):
            return t.reshape(b, s, HEADS, HEAD_DIM).transpose(0, 2, 1, 3)
        q = split_heads(x @ Wq.T)
        k = split_heads(x @ Wk.T)
        v = split_heads(x @ Wv.T)
        q = jax.nn.elu(q) + 1.0
        k = jax.nn.elu(k) + 1.0
        kv_state = jnp.einsum('bhnd,bhne->bhde', k, v)
        k_state = k.sum(axis=2)
        attn_out = jnp.einsum('bhnd,bhde->bhne', q, kv_state)
        denom = jnp.maximum(jnp.einsum('bhnd,bhd->bhn', q, k_state), 1e-06)[..., None]
        attn_out = (attn_out / denom).transpose(0, 2, 1, 3).reshape(b, s, d)
        xp = jnp.pad(x, ((0, 0), (1, 1), (0, 0)))
        local = xp[:, :-2, :] * conv_w[:, 0] + xp[:, 1:-1, :] * conv_w[:, 1] + xp[:, 2:, :] * conv_w[:, 2] + conv_b
        return (attn_out + local) @ Wp.T + bp

    def _L0_ffn_ref(x, router_w, router_b, gate_w, up_w, down_w, sh_gate_w, sh_up_w, sh_down_w):
        import jax, jax.numpy as jnp
        import numpy as np
        B, S, D = (4, 256, 128)
        F = 344
        E = 8
        TOPK = 2

        def _ffn(x, gw, uw, dw):
            return jax.nn.silu(x @ gw) * (x @ uw) @ dw
        b, s, d = x.shape
        xt = x.reshape(b * s, d)
        probs = jax.nn.softmax(xt @ router_w + router_b, axis=-1)
        rw, ids = jax.lax.top_k(probs, TOPK)
        rw = rw / (jnp.sum(rw, axis=-1, keepdims=True) + 1e-20)
        y = jnp.zeros_like(xt)
        for e in range(E):
            w_e = jnp.sum(jnp.where(ids == e, rw, 0.0), axis=-1)
            y = y + w_e[:, None] * _ffn(xt, gate_w[e], up_w[e], down_w[e])
        y = y + _ffn(xt, sh_gate_w, sh_up_w, sh_down_w)
        return y.reshape(b, s, d)
    x = L0_attn_x
    xn = _layernorm(x, axis=-1)
    x = x + _L0_attn_ref(xn, L0_attn_Wq, L0_attn_Wk, L0_attn_Wv, L0_attn_Wp, L0_attn_bp, L0_attn_conv_w, L0_attn_conv_b) + _L0_ffn_ref(xn, L0_ffn_router_w, L0_ffn_router_b, L0_ffn_gate_w, L0_ffn_up_w, L0_ffn_down_w, L0_ffn_sh_gate_w, L0_ffn_sh_up_w, L0_ffn_sh_down_w)
    return x

_drawn_inputs = setup_inputs


def setup_inputs(seed=0):
    import zlib

    import numpy as np

    out = dict(_drawn_inputs(seed))
    spreads = {'L0_attn_bp': (0.0, 0.647), 'L0_attn_conv_b': (0.0, 0.572), 'L0_ffn_router_b': (0.0, 0.8)}
    factors = {'L0_attn_Wq': 40.152,
     'L0_ffn_router_w': 8.0,
     'L0_ffn_gate_w': 8.0,
     'L0_ffn_up_w': 8.0,
     'L0_ffn_down_w': 8.0,
     'L0_ffn_sh_gate_w': 8.0,
     'L0_ffn_sh_up_w': 8.0,
     'L0_ffn_sh_down_w': 8.0,
     'L0_attn_Wk': 8.0,
     'L0_attn_Wv': 6.422}
    for name, (base, spread) in spreads.items():
        noise = np.random.default_rng([zlib.crc32(name.encode()), seed]).standard_normal(out[name].shape)
        drawn = base * np.exp(spread * noise) if base else spread * noise
        out[name] = jnp.asarray(drawn.astype(out[name].dtype))
    for name, factor in factors.items():
        out[name] = (out[name] * factor).astype(out[name].dtype)
    return out
```

```python
from contextlib import ExitStack

import numpy as np

import concourse.bass as bass
from concourse import mybir

F32 = mybir.dt.float32
F32R = mybir.dt.float32r
I32 = mybir.dt.int32
ALU = mybir.AluOpType
ACT = mybir.ActivationFunctionType
AX = mybir.AxisListType

P = 128
NORM_VAR = 3


class Turn:

    def __init__(self, n, k, r, least):
        self.n, self.k, self.r, self.least = n, k, r, least

    def past(self, depth):
        if isinstance(self.n, int):
            return self.n >= depth
        assert self.least >= depth - 1
        return True


def pipeline(eng, total, lag, ring, step, between=None, loop=True):

    def at(s, r, k, least):
        def turn(d):
            if isinstance(s, int):
                n = s - d
                return Turn(n, n % ring, n // ring, n) if 0 <= n < total else None
            return Turn(s - d, (k - d) % ring, r + (k - d) // ring, least - d)
        return turn

    for s in range(ring if loop else total):
        step(at(s, 0, s, s))
        if between and s == 0:
            between()
    if loop:
        rounds(eng, total, ring, step, at)
    for s in range(total, total + lag):
        step(at(s, 0, 0, s))


def rounds(eng, total, ring, step, at):
    with eng.Fori(1, total // ring) as r:
        for k in range(ring):
            step(at(r * ring + k, r, k, ring + k))


class Chain:

    def __init__(self, eng, sem, start=0):
        self.eng, self.sem, self.n = eng, sem, start

    def link(self, ins):
        self.n = self.n + 1
        ins.then_inc(self.sem, 1)
        self.eng.wait_ge(self.sem, self.n)


def build(nc, x, wqT, wkvT, wpT, bp, conv_w, conv_b, router_w, router_b,
          gate_w, up_w, down_w, sh_gate_w, sh_up_w, sh_down_w, out, slots, pair_out):
    B, S, D = x.shape
    NT = B * S // P
    G = 4
    NG = NT // G
    GT = G * P
    BG = GT // S
    TB = S // P
    HEADS = 16
    HD = D // HEADS
    E, _, F = gate_w.shape
    FC = [P, P, F - 2 * P]
    NC = len(FC)
    TILES = NT * 2 + E
    REC = D + 4
    GU = 2 * F
    WCOLS = 2 * GU + NC * 2 * P
    TOK = NT * P
    EPS = 1e-5
    assert D == P and len(FC) == 3 and 0 < FC[2] <= P and TILES % 8 == 0

    with ExitStack() as ctx:
        def sb(name, shape, dt=F32):
            return ctx.enter_context(nc.sbuf_tensor(name, shape, dt))

        def sem(name):
            return ctx.enter_context(nc.semaphore(name))

        acc = sb("acc", [P, NT, D])
        rec = sb("rec", [P, NT, REC])
        xT = sb("xT", [P, NT * P])
        W = sb("W", [P, E + 1, WCOLS], F32R)
        stage = sb("stage", [P, 2, GU + NC * P])
        split = sb("split", [P, 8192], F32R)
        work = sb("work", [P, 8392])
        ident = sb("ident", [P, P])
        head_rows = sb("head_rows", [P, HEADS])
        head_block = sb("head_block", [P, HEADS, HD])
        before = sb("before", [P, P])
        ones = sb("ones", [P, P])
        wq_sb = sb("wq_sb", [P, D])
        wkv_sb = sb("wkv_sb", [P, 2 * D])
        wp_sb = sb("wp_sb", [P, D])
        router_sb = sb("router_sb", [P, E])
        rbias = sb("rbias", [P, E])
        bpb = sb("bpb", [P, D])
        cw = sb("cw", [P, 3])
        cb = sb("cb", [P, 1])
        pad = sb("pad", [P, REC])
        slot_id = sb("slot_id", [P, TILES])
        same_expert = sb("same_expert", [P, E, NT])
        expert_id = sb("expert_id", [P, E])
        tile_expert = sb("tile_expert", [P, TILES], I32)
        slot_lo = sb("slot_lo", [P, NT], I32)
        slot_hi = sb("slot_hi", [P, NT], I32)
        tile_no = sb("tile_no", [P, TILES])
        mv = sb("mv", [P, NT, 2])
        small = sb("small", [P, 14, NT])
        cols = sb("cols", [P, 6, E])
        counts_i = sb("counts_i", [P, 2, E], I32)
        dest = sb("dest", [P, 8], I32)
        wslot = sb("wslot", [P, 8])
        meta = sb("meta", [P, 6, 4])

        def area(base):
            at = [0]

            def take(*shape):
                n = 1
                for d in shape:
                    n *= d
                v = base[:, at[0]:at[0] + n]
                at[0] += n
                if len(shape) == 2:
                    return v.rearrange("p (a b) -> p a b", a=shape[0])
                return v
            return take


        def area(base):
            at = [0]

            def take(*shape):
                n = int(np.prod(shape))
                v = base[:, at[0]:at[0] + n]
                at[0] += n
                if len(shape) == 2:
                    return v.rearrange("p (a b) -> p a b", a=shape[0])
                return v
            return take

        take = area(work)
        xr = take(2, GT)
        relu_q = take(GT)
        relu_k = take(GT)
        qT = take(2, GT)
        kb = take(2 * G, D)
        vb = take(2 * G, D + 1)
        den = take(G, HEADS)
        rden = take(G, HEADS)
        routing_at = 4 * 2 * GT + 2 * G * (D + 1) + 2 * G * HEADS
        kvm = take(2 * BG, D + HEADS)
        attn = take(G, D)
        loc = take(2, GT)
        atT = take(2, GT)
        take = area(work[:, routing_at:])
        L = take(NT, E)
        ex = take(NT, E)
        first = take(NT, E)
        second = take(NT, E)
        chosen = take(NT, E)
        L2 = take(NT, E)
        tmp = take(NT, E)
        totals = take(E, NT)
        upto = take(E, NT)
        pos = take(NT, E)
        stats = work[:, routing_at:routing_at + NT * 6].rearrange("p (t s) -> p t s", s=6)
        lgT = qT[0:E, :, :]
        take = area(work)
        silu_s = take(2, GT)
        h_s = take(2, GT)
        y_s = take(G, D)
        take = area(work)
        FP = NC * P
        silu_e = take(2, F)
        h_e = take(2, FP)
        y_half = take(2, D)
        y_buf = take(4, D)
        xs = stage[:, :, :].rearrange("p a b -> p (a b)")[:, 0:8 * REC].rearrange("p (t w) -> p t w", w=REC)
        take = area(split)
        xh_s = take(2, GT)
        xl_s = take(2, GT)
        hh_s = take(2 * NC, GT)
        hl_s = take(2 * NC, GT)
        take = area(split)
        xh_e = take(2, D)
        xl_e = take(2, D)
        hh_e = take(2, FP)
        hl_e = take(2, FP)

        def w_gu(e, part, which):
            a = part * GU + which * F
            return W[:, e, a:a + F]

        def w_down(e):
            return W[:, e, 2 * GU:WCOLS].rearrange("p (c w) -> p c w", c=NC)

        PS = ctx.enter_context(nc.psum_tensor("PS", [P, 8, 512], F32))

        consts_in = sem("consts_in")
        x_in = [sem(f"x_in{j}") for j in range(NG)]
        pool_const = sem("pool_const")
        masks_ready = sem("masks_ready")
        pad_ready = sem("pad_ready")
        slots_cleared = sem("slots_cleared")
        stage_in = [sem(f"stage_in{j}") for j in range(2)]
        stage_clear = sem("stage_clear")
        w_high = sem("w_high")
        w_low = sem("w_low")
        ln_step = sem("ln_step")
        std_ready = sem("std_ready")
        xn_ready = sem("xn_ready")
        bias_added = sem("bias_added")
        xT_mm = sem("xT_mm")
        xT_out = sem("xT_out")
        lg_mm = sem("lg_mm")
        lg_out = sem("lg_out")
        logits_mm = sem("logits_mm")
        rt_step = sem("rt_step")
        shifted = sem("shifted")
        exp_ready = sem("exp_ready")
        chosen_ready = sem("chosen_ready")
        counts_mm = sem("counts_mm")
        routed = sem("routed")
        tiles_ready = sem("tiles_ready")
        spread = sem("spread")
        xr_in = [sem(f"xr_in{j}") for j in range(2)]
        q_mm = sem("q_mm")
        kv_mm = sem("kv_mm")
        act_step = sem("act_step")
        q_act = sem("q_act")
        k_act = sem("k_act")
        v_act = sem("v_act")
        q_ready = sem("q_ready")
        k_ready = sem("k_ready")
        state_mm = sem("state_mm")
        kvm_ready = sem("kvm_ready")
        num_mm = sem("num_mm")
        num_step = sem("num_step")
        attn_ready = sem("attn_ready")
        atT_mm = sem("atT_mm")
        loc_act = sem("loc_act")
        conv_step = sem("conv_step")
        loc_ready = sem("loc_ready")
        at_ready = sem("at_ready")
        proj_mm = sem("proj_mm")
        proj_added = sem("proj_added")
        sh_xh = sem("sh_xh")
        sh_xl = sem("sh_xl")
        sh_gu_mm = sem("sh_gu_mm")
        sh_silu = sem("sh_silu")
        sh_h = sem("sh_h")
        sh_hh = sem("sh_hh")
        sh_hl = sem("sh_hl")
        sh_y_mm = sem("sh_y_mm")
        sh_y_act = sem("sh_y_act")
        sh_step = sem("sh_step")
        sh_added = sem("sh_added")
        h_clear = sem("h_clear")
        xs_in = [sem(f"xs_in{j}") for j in range(2)]
        ex_xT_mm = sem("ex_xT_mm")
        ex_xh = sem("ex_xh")
        ex_xl = sem("ex_xl")
        ex_gu_mm = sem("ex_gu_mm")
        ex_silu = sem("ex_silu")
        ex_h = sem("ex_h")
        ex_hT_mm = sem("ex_hT_mm")
        ex_hh = sem("ex_hh")
        ex_hl = sem("ex_hl")
        ex_y_mm = sem("ex_y_mm")
        ex_y_act = sem("ex_y_act")
        meta_step = sem("meta_step")
        meta_ready = sem("meta_ready")
        ex_y = sem("ex_y")
        sends = sem("sends")
        sp_loads = sem("sp_loads")
        y_sent = [sem(f"y_sent{j}") for j in range(4)]
        pair_in = [sem(f"pair_in{j}") for j in range(4)]
        fin_step = sem("fin_step")
        fin_ready = sem("fin_ready")
        stored = sem("stored")

        block = ctx.enter_context(nc.Block())
        x_rows = x.rearrange("b (h p) d -> p (b h) d", p=P)
        out_rows = out.rearrange("b (h p) d -> p (b h) d", p=P)
        slot_rows = slots.rearrange("(t p) w -> p t w", p=P)
        N_CONST = 8

        @block.sync
        def _(sp):
            for g in range(NG):
                sp.dma_start(acc[:, G * g:G * g + G, :], x_rows[:, G * g:G * g + G, :]).then_inc(x_in[g], 16)

            def load_weights(gate, up, down, k):
                sp.dma_start(stage[:, k, 0:F], gate).then_inc(stage_in[k], 16)
                sp.dma_start(stage[:, k, F:GU], up).then_inc(stage_in[k], 16)
                d = stage[:, k, GU:].rearrange("p (c w) -> p c w", c=NC)
                sp.dma_start(d[:, 0:2, :], down[0:2 * P, :].rearrange("(c p) w -> p c w", p=P)).then_inc(stage_in[k], 16)
                sp.dma_start(d[0:FC[2], 2, :], down[2 * P:F, :]).then_inc(stage_in[k], 16)

            sp.wait_ge(stage_clear, 1)
            load_weights(sh_gate_w, sh_up_w, sh_down_w, 0)
            load_weights(gate_w[0], up_w[0], down_w[0], 1)
            sp.wait_ge(pad_ready, 1)
            sp.dma_start(slot_rows, pad[:, :].unsqueeze(1).to_broadcast([P, TILES, REC])).then_inc(slots_cleared, 16)
            for e in range(1, E):
                sp.wait_ge(w_high, e)
                sp.wait_ge(w_low, e)
                load_weights(gate_w[e], up_w[e], down_w[e], (e + 1) % 2)

            def xr_load(turn):
                t = turn(0)
                sp.wait_ge(xT_out, t.n + 1)
                sp.sem_inc(sp_loads, 1)
                if t.past(2):
                    sp.wait_ge(kv_mm, t.n - 1)
                    sp.sem_inc(sp_loads, 1)
                sp.dma_start(xr[:, t.k, :], xT[:, bass.ds(t.n * GT, GT)]).then_inc(xr_in[t.k], 16)
            sp.wait_ge(w_low, E + 1)
            pipeline(sp, NG, 0, 2, xr_load)

            sp.wait_ge(spread, 16 * 2 * NT)

            def xs_load(turn):
                t = turn(0)
                if t.past(2):
                    sp.wait_ge(ex_xT_mm, 4 * t.n - 4)
                    sp.sem_inc(sp_loads, 1)
                    sp.wait_ge(meta_ready, t.n - 1)
                    sp.sem_inc(sp_loads, 1)
                sp.dma_start(xs[:, 4 * t.k:4 * t.k + 4, :],
                             slot_rows[:, bass.ds(t.n * 4, 4), :]).then_inc(xs_in[t.k], 16)
            pipeline(sp, TILES // 4, 0, 2, xs_load)

            for j in range(4):
                sp.wait_ge(y_sent[j], 16 * TILES // 4)
            pair = pair_out.rearrange("(t p) d -> p t d", p=P)
            Q = NT // 4
            for j in range(4):
                sp.dma_start(xT[:, j * Q * P:(j + 1) * Q * P].rearrange("p (t d) -> p t d", d=D),
                             pair[:, j * Q:(j + 1) * Q, :]).then_inc(pair_in[j], 16)
                sp.dma_start(rec[:, j * Q:(j + 1) * Q, 0:D],
                             pair[:, NT + j * Q:NT + (j + 1) * Q, :]).then_inc(pair_in[j], 16)
            for j in range(4):
                sp.wait_ge(fin_ready, j + 1)
                sp.dma_start(out_rows[:, j * Q:(j + 1) * Q, :], acc[:, j * Q:(j + 1) * Q, :]).then_inc(stored, 16)
            sp.wait_ge(stored, 64)

        @block.gpsimd
        def _(pool):
            c = Chain(pool, pool_const)
            pool.memset(stage[:, :, GU + 2 * P:], 0.0).then_inc(stage_clear, 1)
            c.link(pool.memset(ident[:, :], 0.0))
            c.link(pool.affine_select(out=ident[:, :], in_=ident[:, :], compare_op=ALU.not_equal, fill=1.0,
                                      base=0, pattern=[[-1, P]], channel_multiplier=1))
            c.link(pool.memset(pad[:, 0:D], 0.0))
            c.link(pool.memset(pad[:, D:D + 1], float(2 * TOK)))
            c.link(pool.memset(pad[:, D + 1:D + 2], -1.0))
            pool.memset(pad[:, D + 2:REC], 0.0).then_inc(pad_ready, 1)
            pool.memset(ones[:, :], 1.0)
            c.link(pool.memset(head_rows[:, :], 1.0))
            c.link(pool.affine_select(out=head_rows[:, :], in_=head_rows[:, :], compare_op=ALU.is_ge, fill=0.0,
                                      base=0, pattern=[[-HD, HEADS]], channel_multiplier=1))
            c.link(pool.affine_select(out=head_rows[:, :], in_=head_rows[:, :], compare_op=ALU.is_ge, fill=0.0,
                                      base=HD - 1, pattern=[[HD, HEADS]], channel_multiplier=-1))
            pool.tensor_copy(head_block[:, :, :], head_rows[:, :].unsqueeze(2).to_broadcast([P, HEADS, HD]))
            c.link(pool.memset(before[:, :], 1.0))
            c.link(pool.affine_select(out=before[:, :], in_=before[:, :], compare_op=ALU.is_gt, fill=0.0,
                                      base=0, pattern=[[1, P]], channel_multiplier=-1))
            c.link(pool.memset(same_expert[:, :, :], 1.0))
            pool.memset(same_expert[:, :, 0:1], 0.0)
            exact = {"allow_small_or_imprecise_dtypes": True}
            pool.iota(expert_id[:, :], [[1, E]], base=0, channel_multiplier=0, **exact)
            pool.iota(tile_no[:, :], [[1, TILES]], base=0, channel_multiplier=0, **exact)
            pool.iota(slot_id[:, :], [[P, TILES]], base=0, channel_multiplier=1, **exact)
            pool.memset(vb[:, :, D:D + 1], 1.0)
            pool.iota(rec[:, :, D], [[P, NT]], base=0, channel_multiplier=1, **exact).then_inc(masks_ready, 1)
            for n in range(E + 1):
                k, e = n % 2, (n - 1) % (E + 1)
                pool.wait_ge(w_high, n + 1)
                pool.tensor_tensor(W[:, e, GU:2 * GU], stage[:, k, 0:GU], W[:, e, 0:GU].bitcast(F32), ALU.subtract)
                d = w_down(e)
                pool.tensor_tensor(d[:, :, P:2 * P], stage[:, k, GU:].rearrange("p (c w) -> p c w", c=NC),
                                   d[:, :, 0:P].bitcast(F32), ALU.subtract).then_inc(w_low, 1)
            pool.wait_ge(consts_in, 16 * N_CONST)
            pool.wait_ge(xn_ready, NG)
            pool.tensor_tensor(acc[:, :, :], acc[:, :, :], bpb[:, :].unsqueeze(1).to_broadcast([P, NT, D]),
                               ALU.add).then_inc(bias_added, 1)
            pool.wait_ge(routed, 1)
            pool.wait_ge(slots_cleared, 16)
            for t in range(NT):
                for at in (slot_lo, slot_hi):
                    pool.indirect_dma_start(out=slots, out_offset=bass.IndirectOffsetOnAxis(ap=at[:, t:t + 1], axis=0),
                                            in_=rec[:, t, :], in_offset=None).then_inc(spread, 16)

            def send(turn):
                t = turn(0)
                pool.wait_ge(ex_y, t.n + 1)
                pool.sem_inc(sends, 1)
                pool.indirect_dma_start(out=pair_out,
                                        out_offset=bass.IndirectOffsetOnAxis(ap=dest[:, t.k:t.k + 1], axis=0),
                                        in_=y_buf[:, t.k % 4, :], in_offset=None).then_inc(y_sent[t.k % 4], 16)
            pipeline(pool, TILES, 0, 8, send)

        @block.tensor
        def _(pe):
            pe.wait_ge(masks_ready, 1)
            pe.wait_ge(consts_in, 16 * N_CONST)

            def norm_step(turn):
                if t := turn(0):
                    pe.wait_ge(xn_ready, t.n + 1)
                    if t.past(2):
                        pe.wait_ge(xT_out, t.n - 1)
                    for j in range(G):
                        m = nc.tensor.transpose(PS[:, t.k, j * P:(j + 1) * P], rec[:, t.n * G + j, 0:D], ident[:, :])
                    m.then_inc(xT_mm, 1)
                if t := turn(1):
                    pe.wait_ge(xT_out, t.n + 1)
                    if t.past(2):
                        pe.wait_ge(lg_out, t.n - 1)
                    nc.tensor.matmul(PS[0:E, 2 + t.k, :], router_sb[:, :], xT[:, bass.ds(t.n * GT, GT)],
                                     start=True, stop=True).then_inc(lg_mm, 1)
                if t := turn(2):
                    pe.wait_ge(lg_out, t.n + 1)
                    for j in range(G):
                        m = nc.tensor.matmul(PS[:, 4, bass.ds((t.n * G + j) * E, E)], lgT[:, t.k, j * P:(j + 1) * P],
                                             ident[0:E, 0:E], start=True, stop=True)
                    m.then_inc(logits_mm, 1)
            pipeline(pe, NG, 2, 2, norm_step, loop=False)

            def count_tokens():
                pe.wait_ge(chosen_ready, 1)
                m = chosen.rearrange("p t e -> p (t e)")
                nc.tensor.matmul(PS[:, 6, 0:NT * E], before[:, :], m, start=True, stop=True)
                nc.tensor.matmul(PS[:, 6, NT * E:2 * NT * E], ones[:, :], m, start=True, stop=True).then_inc(counts_mm, 1)

            def attention_step(turn):
                if t := turn(0):
                    pe.wait_ge(xr_in[t.k], 16 * (t.r + 1))
                    if t.past(1):
                        pe.wait_ge(v_act, t.n)
                    nc.tensor.matmul(PS[:, 0, :], wq_sb[:, :], xr[:, t.k, :], start=True, stop=True).then_inc(q_mm, 1)
                    for j in range(G):
                        m = nc.tensor.matmul(PS[:, 1 + j // 2, (j % 2) * 2 * D:(j % 2 + 1) * 2 * D],
                                             xr[:, t.k, j * P:(j + 1) * P], wkv_sb[:, :], start=True, stop=True)
                    m.then_inc(kv_mm, 1)
                if t := turn(2):
                    pe.wait_ge(attn_ready, t.n + 1)
                    if t.past(1):
                        pe.wait_ge(at_ready, t.n)
                    for j in range(G):
                        m = nc.tensor.transpose(PS[:, 6, j * P:(j + 1) * P], attn[:, j, :], ident[:, :])
                    m.then_inc(atT_mm, 1)
                if t := turn(1):
                    pe.wait_ge(k_ready, t.n + 1)
                    pe.wait_ge(v_act, t.n + 1)
                    if t.past(1):
                        pe.wait_ge(kvm_ready, t.n)
                    for j in range(G):
                        b, i = j // TB, j % TB
                        m = nc.tensor.matmul(PS[:, 3, b * (D + 1):(b + 1) * (D + 1)], kb[:, t.k * G + j, :],
                                             vb[:, t.k * G + j, :], start=(i == 0), stop=(i == TB - 1))
                    m.then_inc(state_mm, 1)
                if t := turn(2):
                    pe.wait_ge(at_ready, t.n + 1)
                    if t.past(1):
                        pe.wait_ge(proj_added, t.n)
                    for j in range(G):
                        m = nc.tensor.matmul(PS[:, 7, j * D:(j + 1) * D], atT[:, t.k, j * P:(j + 1) * P], wp_sb[:, :],
                                             start=True, stop=True)
                    m.then_inc(proj_mm, 1)
                if t := turn(1):
                    pe.wait_ge(kvm_ready, t.n + 1)
                    pe.wait_ge(q_ready, t.n + 1)
                    if t.past(1):
                        pe.wait_ge(attn_ready, t.n)
                    for j in range(G):
                        w = D + HEADS
                        m = nc.tensor.matmul(PS[:, 4 + j // 2, (j % 2) * w:(j % 2 + 1) * w],
                                             qT[:, t.k, j * P:(j + 1) * P], kvm[:, t.k * BG + j // TB, :],
                                             start=True, stop=True)
                    m.then_inc(num_mm, 1)
            pipeline(pe, NG, 2, 2, attention_step, between=count_tokens)

            pe.wait_ge(w_low, E + 1)

            def products(out_ap, left, right):
                (lh, ll), (rh, rl) = left, right
                nc.tensor.matmul(out_ap, lh, rh, start=True, stop=False)
                nc.tensor.matmul(out_ap, lh, rl, start=False, stop=False)
                return nc.tensor.matmul(out_ap, ll, rh, start=False, stop=True)

            def shared_step(turn):
                gu, y = turn(1), turn(2)
                for c in range(NC):
                    if gu:
                        par = (gu.k + c) % 2
                        if c == 0:
                            pe.wait_ge(sh_xl, gu.n + 1)
                        if gu.past(1) or c >= 2:
                            pe.wait_ge(sh_h, gu.n * NC + c - 1)
                        for which in range(2):
                            a = which * F + c * P
                            m = products(PS[0:FC[c], 2 * which + par, :],
                                         (W[:, E, a:a + FC[c]], W[:, E, GU + a:GU + a + FC[c]]),
                                         (xh_s[:, gu.k, :], xl_s[:, gu.k, :]))
                        m.then_inc(sh_gu_mm, 1)
                    if c == 0 and y:
                        pe.wait_ge(sh_hl, y.n * NC + NC)
                        if y.past(1):
                            pe.wait_ge(sh_added, y.n)
                        for j in range(G):
                            m = down(PS[:, 4 + 2 * y.k + j // 2, (j % 2) * 2 * P:(j % 2 + 1) * 2 * P], w_down(E),
                                     lambda c, h, j=j: (hh_s, hl_s)[h][0:FC[c], y.k * NC + c, j * P:(j + 1) * P])
                        m.then_inc(sh_y_mm, 1)

            def down(out_ap, wd, hidden):
                for c in range(NC):
                    nc.tensor.matmul(out_ap, hidden(c, 0), wd[0:FC[c], c, :], start=(c == 0), stop=False)
                    m = nc.tensor.matmul(out_ap[:, 0:D], hidden(c, 1), wd[0:FC[c], c, 0:P],
                                         start=False, stop=(c == NC - 1))
                return m
            pipeline(pe, NG, 2, 2, shared_step)

            pe.wait_ge(tiles_ready, 1)
            pe.wait_ge(h_clear, 1)

            def expert_of(t):
                return bass.ds(pe.value_load(tile_expert[0:1, bass.ds(t.n, 1)], min_val=0, max_val=E - 1), 1)

            def expert_step(turn):
                if t := turn(0):
                    pe.wait_ge(xs_in[t.k // 4], 16 * (t.r + 1))
                    if t.past(1):
                        pe.wait_ge(ex_xl, t.n)
                    nc.tensor.transpose(PS[:, 6, 0:P], xs[:, t.k, 0:D],
                                        ident[:, :]).then_inc(ex_xT_mm, 1)
                if t := turn(1):
                    w = W[:, expert_of(t), 0:2 * GU].rearrange("p e w -> p (e w)")
                    pe.wait_ge(ex_xl, t.n + 1)
                    if t.past(2):
                        pe.wait_ge(ex_h, t.n - 1)
                    p = t.k % 2
                    g, u = PS[:, p, 0:F], PS[:, 2 + p, 0:F]
                    nc.tensor.matmul(g, xh_e[:, p, :], w[:, 0:F], start=True, stop=False)
                    nc.tensor.matmul(g, xh_e[:, p, :], w[:, GU:GU + F], start=False, stop=False)
                    nc.tensor.matmul(u, xh_e[:, p, :], w[:, F:GU], start=True, stop=False)
                    nc.tensor.matmul(u, xh_e[:, p, :], w[:, GU + F:2 * GU], start=False, stop=False)
                    nc.tensor.matmul(g, xl_e[:, p, :], w[:, 0:F], start=False, stop=True)
                    nc.tensor.matmul(u, xl_e[:, p, :], w[:, F:GU], start=False, stop=True).then_inc(ex_gu_mm, 1)
                if t := turn(2):
                    pe.wait_ge(ex_h, t.n + 1)
                    if t.past(2):
                        pe.wait_ge(ex_hl, t.n - 1)
                    p = t.k % 2
                    for c in range(NC):
                        m = nc.tensor.transpose(PS[:, 4 + p, c * P:(c + 1) * P], h_e[:, p, c * P:(c + 1) * P], ident[:, :])
                    m.then_inc(ex_hT_mm, 1)
                if t := turn(3):
                    wd = W[:, expert_of(t), 2 * GU:WCOLS].rearrange("p e (c w) -> p (e c) w", c=NC)
                    pe.wait_ge(ex_hl, t.n + 1)
                    if t.past(1):
                        pe.wait_ge(ex_y, t.n)
                    p = t.k % 2
                    down(PS[:, 7, 0:2 * P], wd,
                         lambda c, h, p=p: (hh_e, hl_e)[h][0:FC[c], p, c * P:(c + 1) * P]).then_inc(ex_y_mm, 1)
            pipeline(pe, TILES, 3, 8, expert_step)

        @block.scalar
        def _(act):
            for dst, src in ((wq_sb, wqT), (wkv_sb, wkvT), (wp_sb, wpT), (cw, conv_w), (router_sb, router_w)):
                act.dma_start(dst[:, :], src).then_inc(consts_in, 16)
            act.dma_start(cb[:, :], conv_b.unsqueeze(1)).then_inc(consts_in, 16)
            act.dma_start(rbias[:, :], router_b.partition_broadcast(P)).then_inc(consts_in, 16)
            act.dma_start(bpb[:, :], bp.partition_broadcast(P)).then_inc(consts_in, 16)

            for n in range(E + 1):
                k, e = n % 2, (n - 1) % (E + 1)
                act.wait_ge(stage_in[k], 64 * (n // 2 + 1))
                nc.scalar.copy(W[:, e, 0:GU], stage[:, k, 0:GU])
                nc.scalar.copy(w_down(e)[:, :, 0:P],
                               stage[:, k, GU:].rearrange("p (c w) -> p c w", c=NC)).then_inc(w_high, 1)

            act.wait_ge(ln_step, NORM_VAR)
            nc.scalar.activation(small[:, 1, :], small[:, 0, :], ACT.Sqrt).then_inc(std_ready, 1)

            def norm_step(turn):
                if t := turn(0):
                    act.wait_ge(xT_mm, t.n + 1)
                    nc.scalar.copy(xT[:, bass.ds(t.n * GT, GT)], PS[:, t.k, :]).then_inc(xT_out, 1)
                if t := turn(1):
                    act.wait_ge(lg_mm, t.n + 1)
                    if t.past(2):
                        act.wait_ge(logits_mm, t.n - 1)
                    nc.scalar.copy(lgT[:, t.k, :], PS[0:E, 2 + t.k, :]).then_inc(lg_out, 1)
            pipeline(act, NG, 1, 2, norm_step)

            act.wait_ge(shifted, 1)
            nc.scalar.activation(ex, ex, ACT.Exp).then_inc(exp_ready, 1)

            kv_psum = PS[:, 1:3, :].rearrange("p b (t w) -> p (b t) w", w=2 * D)

            def attention_step(turn):
                if t := turn(0):
                    act.wait_ge(q_mm, t.n + 1)
                    if t.past(2):
                        act.wait_ge(num_mm, t.n - 1)
                    nc.scalar.activation(qT[:, t.k, :], PS[:, 0, :], ACT.Relu, scale=-1.0).then_inc(act_step, 1)
                    if t.past(1):
                        act.wait_ge(q_ready, t.n)
                    nc.scalar.activation(relu_q, PS[:, 0, :], ACT.Relu)
                    act.wait_ge(act_step, 2 * t.n + 1)
                    nc.scalar.activation(qT[:, t.k, :], qT[:, t.k, :], ACT.Exp, scale=-1.0).then_inc(q_act, 1)
                    act.wait_ge(kv_mm, t.n + 1)
                    if t.past(2):
                        act.wait_ge(state_mm, t.n - 1)
                    kk = kb[:, t.k * G:(t.k + 1) * G, :]
                    nc.scalar.activation(kk, kv_psum[:, :, 0:D], ACT.Relu, scale=-1.0).then_inc(act_step, 1)
                    if t.past(1):
                        act.wait_ge(k_ready, t.n)
                    nc.scalar.activation(relu_k.rearrange("p (t d) -> p t d", d=D), kv_psum[:, :, 0:D], ACT.Relu)
                    act.wait_ge(act_step, 2 * t.n + 2)
                    nc.scalar.activation(kk, kk, ACT.Exp, scale=-1.0).then_inc(k_act, 1)
                    nc.scalar.copy(vb[:, t.k * G:(t.k + 1) * G, 0:D], kv_psum[:, :, D:2 * D]).then_inc(v_act, 1)
                if t := turn(1):
                    act.wait_ge(routed, 1)
                    if t.past(2):
                        act.wait_ge(at_ready, t.n - 1)
                    nc.scalar.activation(loc[:, t.k, :], xT[:, bass.ds(t.n * GT, GT)], ACT.Identity,
                                         bias=cb[:, 0:1], scale=cw[:, 1:2]).then_inc(loc_act, 1)
            pipeline(act, NG, 1, 2, attention_step)

            act.wait_ge(proj_mm, NG)
            act.wait_ge(w_low, E + 1)
            y_psum = [PS[:, 4 + 2 * k:6 + 2 * k, :].rearrange("p b (t w) -> p (b t) w", w=2 * P) for k in range(2)]

            def shared_step(turn):
                if t := turn(0):
                    if t.past(2):
                        act.wait_ge(sh_gu_mm, NC * (t.n - 1))
                    nc.scalar.copy(xh_s[:, t.k, :], xT[:, bass.ds(t.n * GT, GT)]).then_inc(sh_xh, 1)
                gu, y = turn(1), turn(2)
                for c in range(NC):
                    if gu:
                        par, m = (gu.k + c) % 2, gu.n * NC + c
                        act.wait_ge(sh_gu_mm, m + 1)
                        if gu.past(1) or c >= 2:
                            act.wait_ge(sh_h, m - 1)
                        nc.scalar.activation(silu_s[0:FC[c], par, :], PS[0:FC[c], par, :], ACT.Silu).then_inc(sh_silu, 1)
                        act.wait_ge(sh_h, m + 1)
                        if gu.past(2):
                            act.wait_ge(sh_y_mm, gu.n - 1)
                        nc.scalar.copy(hh_s[0:FC[c], gu.k * NC + c, :], h_s[0:FC[c], par, :]).then_inc(sh_hh, 1)
                    if c == 0 and y:
                        act.wait_ge(sh_y_mm, y.n + 1)
                        if y.past(1):
                            act.wait_ge(sh_added, y.n)
                        nc.scalar.copy(y_s, y_psum[y.k][:, :, P:2 * P]).then_inc(sh_y_act, 1)
            pipeline(act, NG, 2, 2, shared_step)

            act.wait_ge(sh_added, NG)

            def expert_step(turn):
                if t := turn(0):
                    act.wait_ge(ex_xT_mm, t.n + 1)
                    if t.past(2):
                        act.wait_ge(ex_gu_mm, t.n - 1)
                    p = t.k % 2
                    nc.scalar.copy(xh_e[:, p, :], PS[:, 6, 0:P]).then_inc(ex_xh, 1)
                if t := turn(1):
                    p = t.k % 2
                    act.wait_ge(ex_gu_mm, t.n + 1)
                    if t.past(2):
                        act.wait_ge(ex_h, t.n - 1)
                    nc.scalar.activation(silu_e[:, p, :], PS[:, p, 0:F], ACT.Silu).then_inc(ex_silu, 1)
                if t := turn(2):
                    p = t.k % 2
                    act.wait_ge(ex_hT_mm, t.n + 1)
                    if t.past(2):
                        act.wait_ge(ex_y_mm, t.n - 1)
                    nc.scalar.copy(hh_e[:, p, :], PS[:, 4 + p, 0:FP]).then_inc(ex_hh, 1)
                if t := turn(3):
                    p = t.k % 2
                    act.wait_ge(ex_y_mm, t.n + 1)
                    act.wait_ge(meta_ready, 2 * t.r + t.k // 4 + 1)
                    if t.past(2):
                        act.wait_ge(ex_y, t.n - 1)
                    nc.scalar.activation(y_half[:, p, :], PS[:, 7, P:2 * P], ACT.Copy,
                                         scale=wslot[:, t.k:t.k + 1]).then_inc(ex_y_act, 1)
            pipeline(act, TILES, 3, 8, expert_step)

        @block.vector
        def _(dve):
            V = nc.vector
            for g in range(NG):
                dve.wait_ge(x_in[g], 16)
                for j in range(G):
                    m = V.bn_stats(stats[:, g * G + j, :], acc[:, g * G + j, :])
            c = Chain(dve, ln_step)
            c.link(m)
            for t in range(NT):
                m = V.bn_aggr(mv[:, t, :], stats[:, t, :])
            c.link(m)
            veps, std, r, t1, t2, rstd = (small[:, i, :] for i in range(6))
            c.link(V.tensor_scalar(veps, mv[:, :, 1], EPS, None, ALU.add))
            assert c.n == NORM_VAR
            dve.wait_ge(std_ready, 1)
            c.link(V.reciprocal(r, std))
            c.link(V.tensor_tensor(t1, r, r, ALU.mult))
            c.link(V.tensor_tensor(t2, t1, veps, ALU.mult))
            c.link(V.tensor_scalar(t1, t2, -0.5, 1.5, ALU.mult, ALU.add))
            c.link(V.tensor_tensor(rstd, r, t1, ALU.mult))
            with dve.Fori(0, NG) as g:
                for j in range(G):
                    t = g * G + j
                    m = V.tensor_scalar(rec[:, bass.ds(t, 1), 0:D], acc[:, bass.ds(t, 1), :],
                                        mv[:, bass.ds(t, 1), 0], rstd[:, bass.ds(t, 1)], ALU.subtract, ALU.mult)
                m.then_inc(xn_ready, 1)

            c = Chain(dve, rt_step)

            def by_token(v):
                return v.unsqueeze(2).to_broadcast([P, NT, E])

            def by_expert(v):
                return v.unsqueeze(1).to_broadcast([P, NT, E])
            (m1, i1, m2, i2, ssum, rsum, p1, p2, t1, t2, w1, w2, hi, lo) = (small[:, i, :] for i in range(14))
            dve.wait_ge(masks_ready, 1)
            dve.wait_ge(consts_in, 16 * N_CONST)
            dve.wait_ge(logits_mm, NG)
            c.link(V.tensor_tensor(L, PS[:, 4, 0:NT * E].rearrange("p (t e) -> p t e", e=E), by_expert(rbias[:, :]), ALU.add))
            c.link(V.tensor_reduce(m1, L, AX.X, ALU.max))
            V.tensor_tensor(ex, L, by_token(m1), ALU.subtract).then_inc(shifted, 1)

            def largest(values, m, i, mask):
                c.link(V.tensor_tensor(tmp, values, by_token(m), ALU.is_equal))
                c.link(V.tensor_scalar(tmp, tmp, -float(E), float(E), ALU.mult, ALU.add))
                c.link(V.tensor_tensor(tmp, tmp, by_expert(expert_id[:, :]), ALU.add))
                c.link(V.tensor_reduce(i, tmp, AX.X, ALU.min))
                c.link(V.tensor_tensor(mask, by_expert(expert_id[:, :]), by_token(i), ALU.is_equal))
            largest(L, m1, i1, first)
            c.link(V.scalar_tensor_tensor(L2, first, -3.0e38, L, ALU.mult, ALU.add))
            c.link(V.tensor_reduce(m2, L2, AX.X, ALU.max))
            largest(L2, m2, i2, second)
            V.tensor_tensor(chosen, first, second, ALU.add).then_inc(chosen_ready, 1)
            dve.wait_ge(exp_ready, 1)
            c.link(V.tensor_reduce(ssum, ex, AX.X, ALU.add))
            c.link(V.reciprocal(rsum, ssum))
            c.link(V.tensor_tensor(ex, ex, by_token(rsum), ALU.mult))
            for mask, p in ((first, p1), (second, p2)):
                c.link(V.tensor_tensor(tmp, ex, mask, ALU.mult))
                c.link(V.tensor_reduce(p, tmp, AX.X, ALU.add))
            c.link(V.scalar_tensor_tensor(t1, p1, 1e-20, p2, ALU.add, ALU.add))
            c.link(V.reciprocal(t2, t1))
            c.link(V.tensor_tensor(w1, p1, t2, ALU.mult))
            c.link(V.tensor_tensor(w2, p2, t2, ALU.mult))
            c.link(V.tensor_tensor(t1, i1, i2, ALU.is_lt))
            c.link(V.tensor_tensor(t2, i1, i2, ALU.is_gt))
            c.link(V.tensor_tensor(p1, w1, t1, ALU.mult))
            c.link(V.tensor_tensor(p2, w2, t2, ALU.mult))
            c.link(V.tensor_tensor(rec[:, :, D + 2], p1, p2, ALU.add))
            c.link(V.tensor_tensor(p1, w1, t2, ALU.mult))
            c.link(V.tensor_tensor(p2, w2, t1, ALU.mult))
            c.link(V.tensor_tensor(rec[:, :, D + 3], p1, p2, ALU.add))
            dve.wait_ge(counts_mm, 1)
            c.link(V.tensor_copy(totals, PS[:, 6, NT * E:2 * NT * E].rearrange("p (t e) -> p e t", e=E)))
            flat = "p e t -> p (e t)"
            c.link(V.tensor_tensor_scan(upto.rearrange(flat), same_expert[:, :, :].rearrange(flat),
                                        totals.rearrange(flat), 0.0, ALU.mult, ALU.add))
            n_tiles, ends, base = cols[:, 0, :], cols[:, 1, :], cols[:, 2, :]
            c.link(V.tensor_scalar(counts_i[:, 0, :], upto[:, :, NT - 1], float(P - 1), None, ALU.add))
            c.link(V.tensor_single_scalar(counts_i[:, 1, :], counts_i[:, 0, :], P.bit_length() - 1,
                                          ALU.logical_shift_right))
            c.link(V.tensor_copy(n_tiles, counts_i[:, 1, :]))
            c.link(V.tensor_tensor_scan(ends, ones[:, 0:E], n_tiles, 0.0, ALU.mult, ALU.add))
            c.link(V.tensor_tensor(base, ends, n_tiles, ALU.subtract))
            c.link(V.tensor_scalar(base, base, float(P), None, ALU.mult))
            c.link(V.tensor_tensor(upto, upto, totals, ALU.subtract))
            c.link(V.tensor_tensor(upto, upto, base.unsqueeze(2).to_broadcast([P, E, NT]), ALU.add))
            c.link(V.tensor_tensor(pos, PS[:, 6, 0:NT * E].rearrange("p (t e) -> p t e", e=E),
                                   upto.rearrange("p e t -> p t e"), ALU.add))
            c.link(V.tensor_tensor(pos, pos, chosen, ALU.mult))
            c.link(V.tensor_reduce(hi, pos, AX.X, ALU.max))
            c.link(V.tensor_reduce(lo, pos, AX.X, ALU.add))
            c.link(V.tensor_tensor(lo, lo, hi, ALU.subtract))
            V.tensor_copy(rec[:, :, D + 1], hi)
            V.tensor_copy(slot_hi[:, :], hi)
            V.tensor_copy(slot_lo[:, :], lo).then_inc(routed, 1)
            at, nxt = L2.rearrange("p t e -> p (t e)")[:, 0:TILES], L.rearrange("p t e -> p (t e)")[:, 0:TILES]
            c.link(V.tensor_scalar(at, tile_no[:, :], ends[:, 0:1], None, ALU.is_ge))
            for e in range(1, E - 1):
                c.link(V.scalar_tensor_tensor(nxt, tile_no[:, :], ends[:, e:e + 1], at, ALU.is_ge, ALU.add))
                at, nxt = nxt, at
            V.tensor_copy(tile_expert[:, :], at).then_inc(tiles_ready, 1)

            dve.wait_ge(tiles_ready, 1)
            dve.wait_ge(bias_added, 1)
            num_psum = [PS[:, 4 + b, 0:2 * (D + HEADS)].rearrange("p (t w) -> p t w", t=2) for b in range(2)]
            seq = "p (b s) -> p b s"

            def attention_step(turn):
                if t := turn(1):
                    dve.wait_ge(loc_act, t.n + 1)
                    l3 = loc[:, t.k, :].rearrange(seq, s=S)
                    x3 = xT[:, bass.ds(t.n * GT, GT)].rearrange(seq, s=S)
                    V.scalar_tensor_tensor(l3[:, :, 1:S], x3[:, :, 0:S - 1], cw[:, 0:1], l3[:, :, 1:S],
                                           ALU.mult, ALU.add).then_inc(conv_step, 1)
                    dve.wait_ge(conv_step, t.n + 1)
                    V.scalar_tensor_tensor(l3[:, :, 0:S - 1], x3[:, :, 1:S], cw[:, 2:3], l3[:, :, 0:S - 1],
                                           ALU.mult, ALU.add).then_inc(loc_ready, 1)
                if t := turn(2):
                    dve.wait_ge(atT_mm, t.n + 1)
                    dve.wait_ge(loc_ready, t.n + 1)
                    if t.past(1):
                        dve.wait_ge(proj_mm, t.n)
                    V.tensor_tensor(atT[:, t.k, :], PS[:, 6, :], loc[:, t.k, :], ALU.add).then_inc(at_ready, 1)
                if t := turn(0):
                    dve.wait_ge(q_act, t.n + 1)
                    V.tensor_tensor(qT[:, t.k, :], qT[:, t.k, :], relu_q, ALU.add).then_inc(q_ready, 1)
                if t := turn(1):
                    dve.wait_ge(state_mm, t.n + 1)
                    if t.past(2):
                        dve.wait_ge(num_mm, t.n - 1)
                    st = PS[:, 3, 0:BG * (D + 1)].rearrange("p (b w) -> p b w", b=BG)
                    km = kvm[:, t.k * BG:(t.k + 1) * BG, :]
                    V.tensor_tensor(km[:, :, 0:D], st[:, :, 0:D], head_block[:, :, :].rearrange("p h d -> p (h d)")
                                    .unsqueeze(1).to_broadcast([P, BG, D]), ALU.mult)
                    V.tensor_tensor(km[:, :, D:D + HEADS], st[:, :, D:D + 1].to_broadcast([P, BG, HEADS]),
                                    head_rows[:, :].unsqueeze(1).to_broadcast([P, BG, HEADS]), ALU.mult).then_inc(kvm_ready, 1)
                if t := turn(2):
                    dve.wait_ge(proj_mm, t.n + 1)
                    a = acc[:, bass.ds(t.n * G, G), :].rearrange("p t d -> p (t d)")
                    V.tensor_tensor(a, PS[:, 7, :], a, ALU.add).then_inc(proj_added, 1)
                if t := turn(0):
                    dve.wait_ge(k_act, t.n + 1)
                    kk = kb[:, t.k * G:(t.k + 1) * G, :].rearrange("p t d -> p (t d)")
                    V.tensor_tensor(kk, kk, relu_k, ALU.add).then_inc(k_ready, 1)
                if t := turn(1):
                    dve.wait_ge(num_mm, t.n + 1)
                    for b in range(2):
                        m = V.tensor_scalar(den[:, 2 * b:2 * b + 2, :], num_psum[b][:, :, D:D + HEADS], 1e-6, None, ALU.max)
                    m.then_inc(num_step, 1)
                    dve.wait_ge(num_step, 2 * t.n + 1)
                    V.reciprocal(rden, den).then_inc(num_step, 1)
                    dve.wait_ge(num_step, 2 * t.n + 2)
                    if t.past(1):
                        dve.wait_ge(atT_mm, t.n)
                    for b in range(2):
                        m = V.tensor_tensor(attn[:, 2 * b:2 * b + 2, :].rearrange("p t (h d) -> p t h d", d=HD),
                                            num_psum[b][:, :, 0:D].rearrange("p t (h d) -> p t h d", d=HD),
                                            rden[:, 2 * b:2 * b + 2, :].unsqueeze(3).to_broadcast([P, 2, HEADS, HD]),
                                            ALU.mult)
                    m.then_inc(attn_ready, 1)
            pipeline(dve, NG, 2, 2, attention_step)

            def shared_step(turn):
                if t := turn(0):
                    dve.wait_ge(sh_xh, t.n + 1)
                    V.tensor_tensor(xl_s[:, t.k, :], xT[:, bass.ds(t.n * GT, GT)], xh_s[:, t.k, :].bitcast(F32),
                                    ALU.subtract).then_inc(sh_xl, 1)
                gu, y = turn(1), turn(2)
                for c in range(NC):
                    if gu:
                        par, m, f = (gu.k + c) % 2, gu.n * NC + c, FC[c]
                        dve.wait_ge(sh_silu, m + 1)
                        if gu.past(1) or c >= 2:
                            dve.wait_ge(sh_hl, m - 1)
                        V.tensor_tensor(h_s[0:f, par, :], PS[0:f, 2 + par, :], silu_s[0:f, par, :], ALU.mult).then_inc(sh_h, 1)
                        dve.wait_ge(sh_hh, m + 1)
                        V.tensor_tensor(hl_s[0:f, gu.k * NC + c, :], h_s[0:f, par, :],
                                        hh_s[0:f, gu.k * NC + c, :].bitcast(F32), ALU.subtract).then_inc(sh_hl, 1)
                    if c == 0 and y:
                        dve.wait_ge(sh_y_act, y.n + 1)
                        a = acc[:, bass.ds(y.n * G, G), :]
                        V.tensor_tensor(a, PS[:, 4 + 2 * y.k:6 + 2 * y.k, :].rearrange("p b (t w) -> p (b t) w", w=2 * P)[:, :, 0:P],
                                        a, ALU.add).then_inc(sh_step, 1)
                        dve.wait_ge(sh_step, y.n + 1)
                        V.tensor_tensor(a, a, y_s, ALU.add).then_inc(sh_added, 1)
            pipeline(dve, NG, 2, 2, shared_step)

            dve.wait_ge(sh_added, NG)
            V.memset(h_e[:, :, F:FP], 0.0).then_inc(h_clear, 1)
            LINKS = 8

            def slot_data(t):
                dve.wait_ge(xs_in[t.k // 4], 16 * (t.r + 1))
                n0 = (2 * t.r + t.k // 4) * LINKS
                c = Chain(dve, meta_step, n0)
                is_hi, not_hi, a, b, is_pad, d = (meta[:, i, :] for i in range(6))
                m4 = xs[:, t.k:t.k + 4, :]
                token, high, wl, wh = (m4[:, :, D + i] for i in range(4))
                ids = slot_id[:, bass.ds(t.n, 4)]
                c.link(V.tensor_tensor(is_hi, high, ids, ALU.is_equal))
                c.link(V.tensor_tensor(not_hi, high, ids, ALU.not_equal))
                c.link(V.tensor_tensor(a, is_hi, wh, ALU.mult))
                c.link(V.tensor_tensor(b, not_hi, wl, ALU.mult))
                c.link(V.tensor_tensor(wslot[:, t.k:t.k + 4], a, b, ALU.add))
                c.link(V.scalar_tensor_tensor(d, is_hi, float(TOK), token, ALU.mult, ALU.add))
                c.link(V.tensor_scalar(is_pad, high, 0.0, None, ALU.is_lt))
                c.link(V.tensor_tensor(is_pad, is_pad, ids, ALU.mult))
                V.tensor_tensor(dest[:, t.k:t.k + 4], d, is_pad, ALU.add).then_inc(meta_ready, 1)

            def expert_step(turn):
                if t := turn(0):
                    dve.wait_ge(ex_xh, t.n + 1)
                    p = t.k % 2
                    V.tensor_tensor(xl_e[:, p, :], PS[:, 6, 0:P], xh_e[:, p, :].bitcast(F32),
                                    ALU.subtract).then_inc(ex_xl, 1)
                if t := turn(1):
                    p = t.k % 2
                    dve.wait_ge(ex_silu, t.n + 1)
                    if t.past(2):
                        dve.wait_ge(ex_hT_mm, t.n - 1)
                    V.tensor_tensor(h_e[:, p, 0:F], PS[:, 2 + p, 0:F], silu_e[:, p, :], ALU.mult).then_inc(ex_h, 1)
                if t := turn(2):
                    p = t.k % 2
                    dve.wait_ge(ex_hh, t.n + 1)
                    V.tensor_tensor(hl_e[:, p, :], PS[:, 4 + p, 0:FP], hh_e[:, p, :].bitcast(F32),
                                    ALU.subtract).then_inc(ex_hl, 1)
                if t := turn(3):
                    p = t.k % 2
                    if t.k % 4 == 0:
                        slot_data(t)
                    dve.wait_ge(ex_y_act, t.n + 1)
                    if t.past(4):
                        dve.wait_ge(y_sent[t.k % 4], 16 * (2 * t.r + t.k // 4))
                    V.scalar_tensor_tensor(y_buf[:, t.k % 4, :], PS[:, 7, 0:P],
                                           wslot[:, t.k:t.k + 1], y_half[:, p, :], ALU.mult, ALU.add).then_inc(ex_y, 1)
            pipeline(dve, TILES, 3, 8, expert_step)

            Q = NT // 4
            for j in range(4):
                dve.wait_ge(pair_in[j], 32)
                a = acc[:, j * Q:(j + 1) * Q, :]
                V.tensor_tensor(a, a, xT[:, j * Q * P:(j + 1) * Q * P].rearrange("p (t d) -> p t d", d=D),
                                ALU.add).then_inc(fin_step, 1)
                dve.wait_ge(fin_step, j + 1)
                V.tensor_tensor(a, a, rec[:, j * Q:(j + 1) * Q, 0:D], ALU.add).then_inc(fin_ready, 1)


_SHAPES = [("L0_attn_bp", None), ("L0_attn_conv_w", None), ("L0_attn_conv_b", None), ("L0_ffn_router_w", None),
           ("L0_ffn_router_b", None), ("L0_ffn_gate_w", None), ("L0_ffn_up_w", None), ("L0_ffn_down_w", None),
           ("L0_ffn_sh_gate_w", None), ("L0_ffn_sh_up_w", None), ("L0_ffn_sh_down_w", None)]


def kernel(**inputs):
    import concourse.bacc as bacc
    from concourse.bass_utils import run_bass_kernel_spmd

    nc = bacc.Bacc("TRN2", target_bir_lowering=False, num_devices=1)
    arrays = {}

    def dram(name, a):
        a = np.ascontiguousarray(a)
        arrays[name] = a
        return nc.dram_tensor(name, a.shape, mybir.dt.from_np(a.dtype), kind="ExternalInput").ap()

    x = dram("x", inputs["L0_attn_x"])
    wqT = dram("wqT", np.asarray(inputs["L0_attn_Wq"]).T)
    wkvT = dram("wkvT", np.concatenate([np.asarray(inputs["L0_attn_Wk"]).T, np.asarray(inputs["L0_attn_Wv"]).T], axis=1))
    wpT = dram("wpT", np.asarray(inputs["L0_attn_Wp"]).T)
    rest = [dram(name, inputs[name]) for name, _ in _SHAPES]
    out = nc.dram_tensor("out", x.shape, F32, kind="ExternalOutput").ap()
    tokens, d = x.shape[0] * x.shape[1], x.shape[2]
    n_slots = (2 * tokens // P + inputs["L0_ffn_gate_w"].shape[0]) * P
    slots = nc.dram_tensor("slots", (n_slots, d + 4), F32, kind="Internal").ap()
    pair_out = nc.dram_tensor("pair_out", (2 * tokens + n_slots, d), F32, kind="Internal").ap()
    build(nc, x, wqT, wkvT, wpT, *rest, out, slots, pair_out)
    got = run_bass_kernel_spmd(nc, [arrays], core_ids=[0])
    return got.results[0]["out"]
```

```python
from contextlib import ExitStack

import numpy as np

import concourse.bass as bass
from concourse import mybir

F32 = mybir.dt.float32
F32R = mybir.dt.float32r
I32 = mybir.dt.int32
ALU = mybir.AluOpType
ACT = mybir.ActivationFunctionType
AX = mybir.AxisListType

P = 128
BY_ACT = [0, 1, 4, 5]
NORM_VAR = 3


class Turn:

    def __init__(self, n, k, r, least):
        self.n, self.k, self.r, self.least = n, k, r, least

    def past(self, depth):
        if isinstance(self.n, int):
            return self.n >= depth
        assert self.least >= depth
        return True


def pipeline(eng, total, lag, ring, step, between=None, loop=True, peeled=1):

    def at(s, r, k, least):
        def turn(d):
            if isinstance(s, int):
                n = s - d
                return Turn(n, n % ring, n // ring, n) if 0 <= n < total else None
            return Turn(s - d, (k - d) % ring, r + (k - d) // ring, least - d)
        return turn

    for s in range(peeled * ring if loop else total):
        step(at(s, 0, s % ring, s))
        if between and s == 0:
            between()
    if loop:
        with eng.Fori(peeled, total // ring) as r:
            for k in range(ring):
                step(at(r * ring + k, r, k, peeled * ring + k))
    for s in range(total, total + lag):
        step(at(s, 0, s % ring, s))


class Chain:

    def __init__(self, eng, sem, start=0, hold=None):
        self.eng, self.sem, self.n, self.hold = eng, sem, start, hold

    def link(self, ins):
        self.n = self.n + 1
        ins.then_inc(self.sem, 1)
        self.eng.wait_ge(self.sem, self.n)
        if self.hold is not None:
            self.eng.sem_inc(self.hold, 1)


def build(nc, x, wqT, wkvT, wpT, bp, conv_w, conv_b, router_w, router_b,
          gate_w, up_w, down_w, sh_gate_w, sh_up_w, sh_down_w, out, slots, pair_out):
    B, S, D = x.shape
    NT = B * S // P
    G = 4
    NG = NT // G
    GT = G * P
    BG = GT // S
    TB = S // P
    HEADS = 16
    HD = D // HEADS
    E, _, F = gate_w.shape
    FC = [P, P, F - 2 * P]
    NC = len(FC)
    TILES = NT * 2 + E
    REC = D + 4
    LOW, ROW, HIGH = slice(0, 2 + D), slice(2, 2 + D), slice(2, REC)
    GU = 2 * F
    WCOLS = 2 * GU + NC * 2 * P
    TOK = NT * P
    EPS = 1e-5
    assert D == P and len(FC) == 3 and 0 < FC[2] <= P and TILES % 8 == 0

    with ExitStack() as ctx:
        def sb(name, shape, dt=F32):
            return ctx.enter_context(nc.sbuf_tensor(name, shape, dt))

        def sem(name):
            return ctx.enter_context(nc.semaphore(name))

        acc = sb("acc", [P, NT, D])
        rec = sb("rec", [P, NT, REC])
        xT = sb("xT", [P, NT * P])
        W = sb("W", [P, E + 1, WCOLS], F32R)
        stage = sb("stage", [P, 2, GU + NC * P])
        split = sb("split", [P, 8192], F32R)
        work = sb("work", [P, 8392])
        ident = sb("ident", [P, P])
        head_rows = sb("head_rows", [P, HEADS])
        head_block = sb("head_block", [P, HEADS, HD])
        before = sb("before", [P, P])
        ones = sb("ones", [P, P])
        wq_sb = sb("wq_sb", [P, D])
        wkv_sb = sb("wkv_sb", [P, 2 * D])
        wp_sb = sb("wp_sb", [P, D])
        router_sb = sb("router_sb", [P, E])
        rbias = sb("rbias", [P, E])
        bpb = sb("bpb", [P, D])
        cw = sb("cw", [P, 3])
        cb = sb("cb", [P, 1])
        pad = sb("pad", [P, REC])
        slot_id = sb("slot_id", [P, TILES])
        same_expert = sb("same_expert", [P, E, NT])
        expert_id = sb("expert_id", [P, E])
        expert_id_up = sb("expert_id_up", [P, E])
        tile_ends = sb("tile_ends", [P, 2, TILES])
        tile_expert = sb("tile_expert", [P, TILES], I32)
        slot_lo = sb("slot_lo", [P, NT], I32)
        slot_hi = sb("slot_hi", [P, NT], I32)
        tile_no = sb("tile_no", [P, TILES])
        mv = sb("mv", [P, NT, 2])
        small = sb("small", [P, 14, NT])
        cols = sb("cols", [P, 6, E])
        counts_i = sb("counts_i", [P, 2, E], I32)
        dest = sb("dest", [P, 8], I32)
        wslot = sb("wslot", [P, 8])
        meta = sb("meta", [P, 4, 4])

        def area(base):
            at = [0]

            def take(*shape):
                n = int(np.prod(shape))
                v = base[:, at[0]:at[0] + n]
                at[0] += n
                if len(shape) == 2:
                    return v.rearrange("p (a b) -> p a b", a=shape[0])
                return v
            return take

        take = area(work)
        xr = take(2, GT)
        qT = take(2, GT)
        kb = take(2 * G, D)
        vb = take(2 * G, D + 1)
        loc = take(2, GT)
        routing_at = 4 * 2 * GT + 2 * G * (D + 1)
        den = take(G, HEADS)
        rden = take(G, HEADS)
        kvm = take(2 * BG, D + HEADS)
        attn = take(G, D)
        atT = take(2, GT)
        take = area(work[:, routing_at:])
        L = take(NT, E)
        ex = take(NT, E)
        first = take(NT, E)
        second = take(NT, E)
        chosen = take(NT, E)
        L2 = take(NT, E)
        tmp = take(NT, E)
        upto = take(E, NT)
        pos = first
        totals = second.rearrange("p t e -> p (t e)").rearrange("p (e t) -> p e t", e=E)
        stats = work[:, routing_at:routing_at + NT * 6].rearrange("p (t s) -> p t s", s=6)
        take = area(work)
        silu_s = take(2, GT)
        h_s = take(2, GT)
        y_s = take(G, D)
        take = area(work)
        FP = NC * P
        silu_e = take(2, F)
        h_e = take(2, FP)
        y_half = take(2, D)
        y_buf = take(4, D)
        xs = stage[:, :, :].rearrange("p a b -> p (a b)")[:, 0:8 * REC].rearrange("p (t w) -> p t w", w=REC)
        take = area(split)
        xh_s = take(2, GT)
        xl_s = take(2, GT)
        hh_s = take(2 * NC, GT)
        hl_s = take(2 * NC, GT)
        take = area(split)
        xh_e = take(2, D)
        xl_e = take(2, D)
        hh_e = take(2, FP)
        hl_e = take(2, FP)

        def w_gu(e, part, which):
            a = part * GU + which * F
            return W[:, e, a:a + F]

        def w_down(e):
            return W[:, e, 2 * GU:WCOLS].rearrange("p (c w) -> p c w", c=NC)

        PS = ctx.enter_context(nc.psum_tensor("PS", [P, 8, 512], F32))
        kv_psum = PS[:, 1:3, :].rearrange("p b (t w) -> p (b t) w", w=2 * D)

        consts_in = sem("consts_in")
        x_in = [sem(f"x_in{j}") for j in range(NG)]
        pool_const = sem("pool_const")
        masks_ready = sem("masks_ready")
        pad_ready = sem("pad_ready")
        slots_cleared = sem("slots_cleared")
        stage_in = [sem(f"stage_in{j}") for j in range(2)]
        stage_clear = sem("stage_clear")
        w_high = sem("w_high")
        w_high_act = sem("w_high_act")
        w_split = sem("w_split")
        ln_step = sem("ln_step")
        std_ready = sem("std_ready")
        xn_ready = sem("xn_ready")
        bias_added = sem("bias_added")
        xT_mm = sem("xT_mm")
        xT_out = sem("xT_out")
        logits_mm = sem("logits_mm")
        rt_step = sem("rt_step")
        tile_step = sem("tile_step")
        shifted = sem("shifted")
        exp_ready = sem("exp_ready")
        chosen_ready = sem("chosen_ready")
        counts_mm = sem("counts_mm")
        routed = sem("routed")
        tiles_ready = sem("tiles_ready")
        spread = sem("spread")
        xr_in = [sem(f"xr_in{j}") for j in range(2)]
        q_mm = sem("q_mm")
        kv_mm = sem("kv_mm")
        act_step = sem("act_step")
        q_act = sem("q_act")
        k_act = sem("k_act")
        v_act = sem("v_act")
        q_ready = sem("q_ready")
        k_ready = sem("k_ready")
        state_mm = sem("state_mm")
        kvm_ready = sem("kvm_ready")
        num_mm = sem("num_mm")
        num_step = sem("num_step")
        attn_ready = sem("attn_ready")
        atT_mm = sem("atT_mm")
        loc_act = sem("loc_act")
        conv_step = sem("conv_step")
        loc_ready = sem("loc_ready")
        at_ready = sem("at_ready")
        proj_mm = sem("proj_mm")
        proj_added = sem("proj_added")
        sh_xh = sem("sh_xh")
        sh_xl = sem("sh_xl")
        sh_gu_mm = sem("sh_gu_mm")
        sh_silu = sem("sh_silu")
        sh_h = sem("sh_h")
        sh_hh = sem("sh_hh")
        sh_hl = sem("sh_hl")
        sh_y_mm = sem("sh_y_mm")
        sh_y_act = sem("sh_y_act")
        sh_step = sem("sh_step")
        sh_added = sem("sh_added")
        h_clear = sem("h_clear")
        xs_in = [sem(f"xs_in{j}") for j in range(2)]
        ex_xT_mm = sem("ex_xT_mm")
        ex_xh = sem("ex_xh")
        ex_xl = sem("ex_xl")
        ex_gu_mm = sem("ex_gu_mm")
        ex_silu = sem("ex_silu")
        ex_h = sem("ex_h")
        ex_hT_mm = sem("ex_hT_mm")
        ex_hh = sem("ex_hh")
        ex_hl = sem("ex_hl")
        ex_y_mm = sem("ex_y_mm")
        ex_y_act = sem("ex_y_act")
        meta_step = sem("meta_step")
        meta_ready = sem("meta_ready")
        ex_y = sem("ex_y")
        sends = sem("sends")
        sp_loads = sem("sp_loads")
        act_holds = sem("act_holds")
        y_sent = [sem(f"y_sent{j}") for j in range(4)]
        pair_in = [sem(f"pair_in{j}") for j in range(4)]
        fin_step = sem("fin_step")
        fin_ready = sem("fin_ready")
        stored = sem("stored")

        block = ctx.enter_context(nc.Block())
        x_rows = x.rearrange("b (h p) d -> p (b h) d", p=P)
        out_rows = out.rearrange("b (h p) d -> p (b h) d", p=P)
        slot_rows = slots.rearrange("(t p) w -> p t w", p=P)
        N_CONST = 8

        @block.sync
        def _(sp):
            for g in range(NG):
                sp.dma_start(acc[:, G * g:G * g + G, :], x_rows[:, G * g:G * g + G, :]).then_inc(x_in[g], 16)

            def load_weights(gate, up, down, k):
                sp.dma_start(stage[:, k, 0:F], gate).then_inc(stage_in[k], 16)
                sp.dma_start(stage[:, k, F:GU], up).then_inc(stage_in[k], 16)
                d = stage[:, k, GU:].rearrange("p (c w) -> p c w", c=NC)
                sp.dma_start(d[:, 0:2, :], down[0:2 * P, :].rearrange("(c p) w -> p c w", p=P)).then_inc(stage_in[k], 16)
                sp.dma_start(d[0:FC[2], 2, :], down[2 * P:F, :]).then_inc(stage_in[k], 16)

            sp.wait_ge(stage_clear, 1)
            load_weights(sh_gate_w, sh_up_w, sh_down_w, 0)
            load_weights(gate_w[0], up_w[0], down_w[0], 1)
            sp.wait_ge(pad_ready, 1)
            sp.dma_start(slot_rows, pad[:, :].unsqueeze(1).to_broadcast([P, TILES, REC])).then_inc(slots_cleared, 16)
            for e in range(1, E):
                sp.wait_ge(w_split, e)
                load_weights(gate_w[e], up_w[e], down_w[e], (e + 1) % 2)

            sp.wait_ge(w_split, E + 1)
            sp.wait_ge(spread, 16 * 2 * NT)

            def xs_load(turn):
                t = turn(0)
                if t.past(2):
                    sp.wait_ge(ex_xT_mm, 4 * t.n - 4)
                    sp.sem_inc(sp_loads, 1)
                    sp.wait_ge(meta_ready, t.n - 1)
                    sp.sem_inc(sp_loads, 1)
                sp.dma_start(xs[:, 4 * t.k:4 * t.k + 4, :],
                             slot_rows[:, bass.ds(t.n * 4, 4), :]).then_inc(xs_in[t.k], 16)
            pipeline(sp, TILES // 4, 0, 2, xs_load)

            for j in range(4):
                sp.wait_ge(y_sent[j], 16 * TILES // 4)
            pair = pair_out.rearrange("(t p) d -> p t d", p=P)
            Q = NT // 4
            for j in range(4):
                sp.dma_start(xT[:, j * Q * P:(j + 1) * Q * P].rearrange("p (t d) -> p t d", d=D),
                             pair[:, j * Q:(j + 1) * Q, :]).then_inc(pair_in[j], 16)
                sp.dma_start(rec[:, j * Q:(j + 1) * Q, ROW],
                             pair[:, NT + j * Q:NT + (j + 1) * Q, :]).then_inc(pair_in[j], 16)
            for j in range(4):
                sp.wait_ge(fin_ready, j + 1)
                sp.dma_start(out_rows[:, j * Q:(j + 1) * Q, :], acc[:, j * Q:(j + 1) * Q, :]).then_inc(stored, 16)
            sp.wait_ge(stored, 64)

        @block.gpsimd
        def _(pool):
            c = Chain(pool, pool_const)
            pool.memset(stage[:, :, GU + 2 * P:], 0.0).then_inc(stage_clear, 1)
            c.link(pool.memset(ident[:, :], 0.0))
            c.link(pool.affine_select(out=ident[:, :], in_=ident[:, :], compare_op=ALU.not_equal, fill=1.0,
                                      base=0, pattern=[[-1, P]], channel_multiplier=1))
            c.link(pool.memset(pad[:, ROW], 0.0))
            for i in (0, REC - 2):
                c.link(pool.memset(pad[:, i:i + 1], float(TOK)))
                c.link(pool.memset(pad[:, i + 1:i + 2], 0.0))
            pool.sem_inc(pad_ready, 1)
            pool.memset(ones[:, :], 1.0)
            c.link(pool.memset(head_rows[:, :], 1.0))
            c.link(pool.affine_select(out=head_rows[:, :], in_=head_rows[:, :], compare_op=ALU.is_ge, fill=0.0,
                                      base=0, pattern=[[-HD, HEADS]], channel_multiplier=1))
            c.link(pool.affine_select(out=head_rows[:, :], in_=head_rows[:, :], compare_op=ALU.is_ge, fill=0.0,
                                      base=HD - 1, pattern=[[HD, HEADS]], channel_multiplier=-1))
            pool.tensor_copy(head_block[:, :, :], head_rows[:, :].unsqueeze(2).to_broadcast([P, HEADS, HD]))
            c.link(pool.memset(before[:, :], 1.0))
            c.link(pool.affine_select(out=before[:, :], in_=before[:, :], compare_op=ALU.is_gt, fill=0.0,
                                      base=0, pattern=[[1, P]], channel_multiplier=-1))
            c.link(pool.memset(same_expert[:, :, :], 1.0))
            pool.memset(same_expert[:, :, 0:1], 0.0)
            exact = {"allow_small_or_imprecise_dtypes": True}
            pool.iota(expert_id[:, :], [[1, E]], base=0, channel_multiplier=0, **exact)
            pool.iota(expert_id_up[:, :], [[1, E]], base=E, channel_multiplier=0, **exact)
            pool.iota(tile_no[:, :], [[1, TILES]], base=0, channel_multiplier=0, **exact)
            pool.iota(slot_id[:, :], [[P, TILES]], base=0, channel_multiplier=1, **exact)
            pool.memset(vb[:, :, D:D + 1], 1.0)
            pool.iota(rec[:, :, 0], [[P, NT]], base=-TOK, channel_multiplier=1, **exact)
            pool.iota(rec[:, :, REC - 2], [[P, NT]], base=0, channel_multiplier=1, **exact).then_inc(masks_ready, 1)
            by_pool = 0
            for n in range(E + 1):
                if n == 4:
                    pool.wait_ge(consts_in, 16 * N_CONST)
                    pool.wait_ge(xn_ready, NG)
                    pool.tensor_tensor(acc[:, :, :], acc[:, :, :], bpb[:, :].unsqueeze(1).to_broadcast([P, NT, D]),
                                       ALU.add).then_inc(bias_added, 1)
                k, e = n % 2, (n - 1) % (E + 1)
                pool.wait_ge(stage_in[k], 64 * (n // 2 + 1))
                d, d_in = w_down(e), stage[:, k, GU:].rearrange("p (c w) -> p c w", c=NC)
                if n in BY_ACT:
                    pool.wait_ge(w_high_act, BY_ACT.index(n) + 1)
                else:
                    pool.tensor_copy(W[:, e, 0:GU], stage[:, k, 0:GU])
                    pool.tensor_copy(d[:, :, 0:P], d_in).then_inc(w_high, 1)
                    by_pool += 1
                    pool.wait_ge(w_high, by_pool)
                pool.tensor_tensor(W[:, e, GU:2 * GU], stage[:, k, 0:GU], W[:, e, 0:GU].bitcast(F32), ALU.subtract)
                pool.tensor_tensor(d[:, :, P:2 * P], d_in, d[:, :, 0:P].bitcast(F32), ALU.subtract).then_inc(w_split, 1)
            pool.wait_ge(routed, 1)
            pool.wait_ge(slots_cleared, 16)
            for t in range(NT):
                for at, part in ((slot_lo, LOW), (slot_hi, HIGH)):
                    pool.indirect_dma_start(out=slots.rearrange("n (a b) -> (n a) b", b=2), out_offset=bass.IndirectOffsetOnAxis(ap=at[:, t:t + 1], axis=0),
                                            in_=rec[:, t, part], in_offset=None).then_inc(spread, 16)

            def slot_data(t):
                pool.wait_ge(xs_in[t.k], 16 * (t.r + 1))
                if t.past(2):
                    for j in range(4):
                        pool.wait_ge(y_sent[j], 16 * (t.n - 1))
                        pool.sem_inc(sends, 1)
                c = Chain(pool, meta_step, t.n * 4, hold=sends)
                four = slice(4 * t.k, 4 * t.k + 4)
                m4 = xs[:, four, :]
                place, none = meta[:, 2 * t.k, :], meta[:, 2 * t.k + 1, :]
                pool.tensor_tensor(wslot[:, four], m4[:, :, 1], m4[:, :, REC - 1], ALU.add)
                c.link(pool.tensor_tensor(place, m4[:, :, 0], m4[:, :, REC - 2], ALU.add))
                c.link(pool.tensor_single_scalar(none, place, float(2 * TOK), ALU.is_ge))
                c.link(pool.tensor_tensor(none, none, slot_id[:, bass.ds(t.n * 4, 4)], ALU.mult))
                c.link(pool.tensor_tensor(place, place, none, ALU.add))
                pool.tensor_copy(dest[:, four], place).then_inc(meta_ready, 1)

            def send_step(turn):
                ahead, t = turn(0), turn(1)
                if t:
                    pool.wait_ge(meta_ready, t.n + 1)
                    pool.sem_inc(sends, 1)
                for j in range(4):
                    if ahead and j == 2:
                        slot_data(ahead)
                    if t:
                        pool.wait_ge(ex_y, 4 * t.n + j + 1)
                        pool.sem_inc(sends, 1)
                        k = 4 * t.k + j
                        pool.indirect_dma_start(out=pair_out,
                                                out_offset=bass.IndirectOffsetOnAxis(ap=dest[:, k:k + 1], axis=0),
                                                in_=y_buf[:, j, :], in_offset=None).then_inc(y_sent[j], 16)
            pipeline(pool, TILES // 4, 1, 2, send_step)

        @block.tensor
        def _(pe):
            pe.wait_ge(masks_ready, 1)
            pe.wait_ge(consts_in, 16 * N_CONST)

            def norm_step(turn):
                if t := turn(0):
                    pe.wait_ge(xn_ready, t.n + 1)
                    if t.past(2):
                        pe.wait_ge(xT_out, t.n - 1)
                    for j in range(G):
                        m = nc.tensor.transpose(PS[:, t.k, j * P:(j + 1) * P], rec[:, t.n * G + j, ROW], ident[:, :])
                    m.then_inc(xT_mm, 1)
                if t := turn(1):
                    pe.wait_ge(xT_out, t.n + 1)
                    for j in range(t.n * G, t.n * G + G):
                        m = nc.tensor.matmul(PS[:, 4, j * E:(j + 1) * E], xT[:, j * P:(j + 1) * P], router_sb[:, :],
                                             start=True, stop=True)
                    m.then_inc(logits_mm, 1)
            pipeline(pe, NG, 1, 2, norm_step, loop=False)

            def count_tokens():
                pe.wait_ge(chosen_ready, 1)
                m = chosen.rearrange("p t e -> p (t e)")
                nc.tensor.matmul(PS[:, 6, 0:NT * E], before[:, :], m, start=True, stop=True)
                nc.tensor.matmul(PS[:, 6, NT * E:2 * NT * E], ones[:, :], m, start=True, stop=True).then_inc(counts_mm, 1)

            def attention_step(turn):
                if t := turn(0):
                    pe.wait_ge(xr_in[t.k], 16 * (t.r + 1))
                    if t.past(1):
                        pe.wait_ge(q_ready, t.n)
                    nc.tensor.matmul(PS[:, 0, :], wq_sb[:, :], xr[:, t.k, :], start=True, stop=True).then_inc(q_mm, 1)
                    if t.past(1):
                        pe.wait_ge(k_ready, t.n)
                    for j in range(G):
                        m = nc.tensor.matmul(PS[:, 1 + j // 2, (j % 2) * 2 * D:(j % 2 + 1) * 2 * D],
                                             xr[:, t.k, j * P:(j + 1) * P], wkv_sb[:, :], start=True, stop=True)
                    m.then_inc(kv_mm, 1)
                if t := turn(1):
                    pe.wait_ge(k_ready, t.n + 1)
                    pe.wait_ge(v_act, t.n + 1)
                    if t.past(1):
                        pe.wait_ge(kvm_ready, t.n)
                    for j in range(G):
                        b, i = j // TB, j % TB
                        m = nc.tensor.matmul(PS[:, 3, b * (D + 1):(b + 1) * (D + 1)], kb[:, t.k * G + j, :],
                                             vb[:, t.k * G + j, :], start=(i == 0), stop=(i == TB - 1))
                    m.then_inc(state_mm, 1)
                if t := turn(2):
                    pe.wait_ge(attn_ready, t.n + 1)
                    if t.past(1):
                        pe.wait_ge(at_ready, t.n)
                    for j in range(G):
                        m = nc.tensor.transpose(PS[:, 6, j * P:(j + 1) * P], attn[:, j, :], ident[:, :])
                    m.then_inc(atT_mm, 1)
                if t := turn(1):
                    pe.wait_ge(kvm_ready, t.n + 1)
                    pe.wait_ge(q_ready, t.n + 1)
                    if t.past(1):
                        pe.wait_ge(attn_ready, t.n)
                    for j in range(G):
                        w = D + HEADS
                        m = nc.tensor.matmul(PS[:, 4 + j // 2, (j % 2) * w:(j % 2 + 1) * w],
                                             qT[:, t.k, j * P:(j + 1) * P], kvm[:, t.k * BG + j // TB, :],
                                             start=True, stop=True)
                    m.then_inc(num_mm, 1)
                if t := turn(2):
                    pe.wait_ge(at_ready, t.n + 1)
                    if t.past(1):
                        pe.wait_ge(proj_added, t.n)
                    for j in range(G):
                        m = nc.tensor.matmul(PS[:, 7, j * D:(j + 1) * D], atT[:, t.k, j * P:(j + 1) * P], wp_sb[:, :],
                                             start=True, stop=True)
                    m.then_inc(proj_mm, 1)
            pipeline(pe, NG, 2, 2, attention_step, between=count_tokens, peeled=2)

            pe.wait_ge(w_split, 1)

            def products(out_ap, left, right):
                (lh, ll), (rh, rl) = left, right
                nc.tensor.matmul(out_ap, lh, rh, start=True, stop=False)
                nc.tensor.matmul(out_ap, lh, rl, start=False, stop=False)
                return nc.tensor.matmul(out_ap, ll, rh, start=False, stop=True)

            def shared_step(turn):
                gu, y = turn(1), turn(2)
                for c in range(NC):
                    if gu:
                        par = (gu.k + c) % 2
                        if c == 0:
                            pe.wait_ge(sh_xl, gu.n + 1)
                        if gu.past(1) or c >= 2:
                            pe.wait_ge(sh_h, gu.n * NC + c - 1)
                        for which in range(2):
                            a = which * F + c * P
                            m = products(PS[0:FC[c], 2 * which + par, :],
                                         (W[:, E, a:a + FC[c]], W[:, E, GU + a:GU + a + FC[c]]),
                                         (xh_s[:, gu.k, :], xl_s[:, gu.k, :]))
                        m.then_inc(sh_gu_mm, 1)
                    if c == NC - 1 and y:
                        pe.wait_ge(sh_hl, y.n * NC + NC)
                        if y.past(2):
                            pe.wait_ge(sh_added, y.n - 1)
                        for j in range(G):
                            m = down(PS[:, 4 + 2 * y.k + j // 2, (j % 2) * 2 * P:(j % 2 + 1) * 2 * P], w_down(E),
                                     lambda c, h, j=j: (hh_s, hl_s)[h][0:FC[c], y.k * NC + c, j * P:(j + 1) * P])
                        m.then_inc(sh_y_mm, 1)

            def down(out_ap, wd, hidden):
                for c in range(NC):
                    nc.tensor.matmul(out_ap, hidden(c, 0), wd[0:FC[c], c, :], start=(c == 0), stop=False)
                    m = nc.tensor.matmul(out_ap[:, 0:D], hidden(c, 1), wd[0:FC[c], c, 0:P],
                                         start=False, stop=(c == NC - 1))
                return m
            pipeline(pe, NG, 2, 2, shared_step, peeled=2)

            pe.wait_ge(tiles_ready, 1)
            pe.wait_ge(w_split, E + 1)
            pe.wait_ge(h_clear, 1)

            def experts_of(first):
                return list(nc.values_load_multi_w_load_instructions(
                    tile_expert[0:1, bass.ds(first, 4)], engines=(mybir.EngineType.PE,), min_val=0, max_val=E - 1,
                    skip_runtime_bounds_check_because="a count of seven comparisons")[1])

            known = {}

            def expert_step(turn):
                if t := turn(1):
                    if t.k == 7:
                        known.update(enumerate(experts_of(t.n - 3), 4))
                    if t.k % 4 == 0:
                        known.update(enumerate(experts_of(t.n), t.k))
                if t := turn(0):
                    pe.wait_ge(xs_in[t.k // 4], 16 * (t.r + 1))
                    if t.past(1):
                        pe.wait_ge(ex_xl, t.n)
                    nc.tensor.transpose(PS[:, 6, 0:P], xs[:, t.k, ROW],
                                        ident[:, :]).then_inc(ex_xT_mm, 1)
                if t := turn(1):
                    w = W[:, bass.ds(known[t.k], 1), 0:2 * GU].rearrange("p e w -> p (e w)")
                    pe.wait_ge(ex_xl, t.n + 1)
                    if t.past(2):
                        pe.wait_ge(ex_h, t.n - 1)
                    p = t.k % 2
                    g, u = PS[:, p, 0:F], PS[:, 2 + p, 0:F]
                    nc.tensor.matmul(g, xh_e[:, p, :], w[:, 0:F], start=True, stop=False)
                    nc.tensor.matmul(g, xh_e[:, p, :], w[:, GU:GU + F], start=False, stop=False)
                    nc.tensor.matmul(u, xh_e[:, p, :], w[:, F:GU], start=True, stop=False)
                    nc.tensor.matmul(u, xh_e[:, p, :], w[:, GU + F:2 * GU], start=False, stop=False)
                    nc.tensor.matmul(g, xl_e[:, p, :], w[:, 0:F], start=False, stop=True)
                    nc.tensor.matmul(u, xl_e[:, p, :], w[:, F:GU], start=False, stop=True).then_inc(ex_gu_mm, 1)
                if t := turn(2):
                    pe.wait_ge(ex_h, t.n + 1)
                    if t.past(2):
                        pe.wait_ge(ex_hl, t.n - 1)
                    p = t.k % 2
                    for c in range(NC):
                        m = nc.tensor.transpose(PS[:, 4 + p, c * P:(c + 1) * P], h_e[:, p, c * P:(c + 1) * P], ident[:, :])
                    m.then_inc(ex_hT_mm, 1)
                if t := turn(3):
                    wd = W[:, bass.ds(known[t.k], 1), 2 * GU:WCOLS].rearrange("p e (c w) -> p (e c) w", c=NC)
                    pe.wait_ge(ex_hl, t.n + 1)
                    if t.past(1):
                        pe.wait_ge(ex_y, t.n)
                    p = t.k % 2
                    down(PS[:, 7, 0:2 * P], wd,
                         lambda c, h, p=p: (hh_e, hl_e)[h][0:FC[c], p, c * P:(c + 1) * P]).then_inc(ex_y_mm, 1)
            pipeline(pe, TILES, 3, 8, expert_step)

        @block.scalar
        def _(act):
            for dst, src in ((wq_sb, wqT), (wkv_sb, wkvT), (wp_sb, wpT), (cw, conv_w), (router_sb, router_w)):
                act.dma_start(dst[:, :], src).then_inc(consts_in, 16)
            act.dma_start(cb[:, :], conv_b.unsqueeze(1)).then_inc(consts_in, 16)
            act.dma_start(rbias[:, :], router_b.partition_broadcast(P)).then_inc(consts_in, 16)
            act.dma_start(bpb[:, :], bp.partition_broadcast(P)).then_inc(consts_in, 16)

            def high_parts(turns):
                for n in turns:
                    act.wait_ge(stage_in[n % 2], 64 * (n // 2 + 1))
                    e = (n - 1) % (E + 1)
                    nc.scalar.copy(W[:, e, 0:GU], stage[:, n % 2, 0:GU])
                    nc.scalar.copy(w_down(e)[:, :, 0:P],
                                   stage[:, n % 2, GU:].rearrange("p (c w) -> p c w", c=NC)).then_inc(w_high_act, 1)
            high_parts(BY_ACT[:2])

            act.wait_ge(ln_step, NORM_VAR)
            nc.scalar.activation(small[:, 1, :], small[:, 0, :], ACT.Sqrt).then_inc(std_ready, 1)

            def norm_step(turn):
                if t := turn(0):
                    act.wait_ge(xT_mm, t.n + 1)
                    nc.scalar.copy(xT[:, bass.ds(t.n * GT, GT)], PS[:, t.k, :]).then_inc(xT_out, 1)
            pipeline(act, NG, 0, 2, norm_step)
            high_parts(BY_ACT[2:])

            act.wait_ge(shifted, 1)
            nc.scalar.activation(ex, ex, ACT.Exp).then_inc(exp_ready, 1)
            act.wait_ge(shifted, 2)
            nc.scalar.activation(small[:, 5, :], small[:, 5, :], ACT.Exp).then_inc(exp_ready, 1)

            def attention_step(turn):
                if t := turn(1):
                    act.wait_ge(q_mm, t.n + 1)
                    if t.past(2):
                        act.wait_ge(num_mm, t.n - 1)
                    nc.scalar.activation(qT[:, t.k, :], PS[:, 0, :], ACT.Relu, scale=-1.0).then_inc(act_step, 1)
                    act.wait_ge(act_step, 2 * t.n + 1)
                    nc.scalar.activation(qT[:, t.k, :], qT[:, t.k, :], ACT.Exp, scale=-1.0).then_inc(q_act, 1)
                    act.wait_ge(kv_mm, t.n + 1)
                    if t.past(2):
                        act.wait_ge(state_mm, t.n - 1)
                    kk = kb[:, t.k * G:(t.k + 1) * G, :]
                    nc.scalar.activation(kk, kv_psum[:, :, 0:D], ACT.Relu, scale=-1.0).then_inc(act_step, 1)
                    nc.scalar.copy(vb[:, t.k * G:(t.k + 1) * G, 0:D], kv_psum[:, :, D:2 * D]).then_inc(v_act, 1)
                    act.wait_ge(act_step, 2 * t.n + 2)
                    nc.scalar.activation(kk, kk, ACT.Exp, scale=-1.0).then_inc(k_act, 1)
                if t := turn(0):
                    act.dma_start(xr[:, t.k, :], xT[:, bass.ds(t.n * GT, GT)]).then_inc(xr_in[t.k], 16)
                if t := turn(1):
                    if t.past(2):
                        act.wait_ge(at_ready, t.n - 1)
                        act.sem_inc(act_holds, 1)
                    nc.scalar.activation(loc[:, t.k, :], xT[:, bass.ds(t.n * GT, GT)], ACT.Identity,
                                         bias=cb[:, 0:1], scale=cw[:, 1:2]).then_inc(loc_act, 1)
            act.wait_ge(xT_out, NG)
            pipeline(act, NG, 1, 2, attention_step, peeled=2)

            act.wait_ge(proj_mm, NG)
            y_psum = [PS[:, 4 + 2 * k:6 + 2 * k, :].rearrange("p b (t w) -> p (b t) w", w=2 * P) for k in range(2)]

            def shared_step(turn):
                if t := turn(3):
                    act.wait_ge(sh_y_mm, t.n + 1)
                    if t.past(1):
                        act.wait_ge(sh_added, t.n)
                    nc.scalar.copy(y_s, y_psum[t.k][:, :, P:2 * P]).then_inc(sh_y_act, 1)
                gu, before_gu = turn(1), turn(2)
                for c in range(NC):
                    if gu:
                        par, m = (gu.k + c) % 2, gu.n * NC + c
                        act.wait_ge(sh_gu_mm, m + 1)
                        if gu.past(1) or c >= 2:
                            act.wait_ge(sh_h, m - 1)
                        nc.scalar.activation(silu_s[0:FC[c], par, :], PS[0:FC[c], par, :], ACT.Silu).then_inc(sh_silu, 1)
                    t, c1 = (gu, c - 1) if c else (before_gu, NC - 1)
                    if t:
                        act.wait_ge(sh_h, t.n * NC + c1 + 1)
                        if t.past(2):
                            act.wait_ge(sh_y_mm, t.n - 1)
                        nc.scalar.copy(hh_s[0:FC[c1], t.k * NC + c1, :], h_s[0:FC[c1], (t.k + c1) % 2, :]).then_inc(sh_hh, 1)
                    if c == 0 and (t := turn(0)):
                        if t.past(2):
                            act.wait_ge(sh_gu_mm, NC * (t.n - 1))
                        nc.scalar.copy(xh_s[:, t.k, :], xT[:, bass.ds(t.n * GT, GT)]).then_inc(sh_xh, 1)
            pipeline(act, NG, 3, 2, shared_step, peeled=2)

            act.wait_ge(sh_added, NG)

            def expert_step(turn):
                if t := turn(0):
                    act.wait_ge(ex_xT_mm, t.n + 1)
                    if t.past(2):
                        act.wait_ge(ex_gu_mm, t.n - 1)
                    p = t.k % 2
                    nc.scalar.copy(xh_e[:, p, :], PS[:, 6, 0:P]).then_inc(ex_xh, 1)
                if t := turn(1):
                    p = t.k % 2
                    act.wait_ge(ex_gu_mm, t.n + 1)
                    if t.past(2):
                        act.wait_ge(ex_h, t.n - 1)
                    nc.scalar.activation(silu_e[:, p, :], PS[:, p, 0:F], ACT.Silu).then_inc(ex_silu, 1)
                if t := turn(2):
                    p = t.k % 2
                    act.wait_ge(ex_hT_mm, t.n + 1)
                    if t.past(2):
                        act.wait_ge(ex_y_mm, t.n - 1)
                    nc.scalar.copy(hh_e[:, p, :], PS[:, 4 + p, 0:FP]).then_inc(ex_hh, 1)
                if t := turn(3):
                    p = t.k % 2
                    act.wait_ge(ex_y_mm, t.n + 1)
                    act.wait_ge(meta_ready, 2 * t.r + t.k // 4 + 1)
                    if t.past(2):
                        act.wait_ge(ex_y, t.n - 1)
                    nc.scalar.activation(y_half[:, p, :], PS[:, 7, P:2 * P], ACT.Copy,
                                         scale=wslot[:, t.k:t.k + 1]).then_inc(ex_y_act, 1)
            pipeline(act, TILES, 3, 8, expert_step)

        @block.vector
        def _(dve):
            V = nc.vector
            for g in range(NG):
                dve.wait_ge(x_in[g], 16)
                for j in range(G):
                    m = V.bn_stats(stats[:, g * G + j, :], acc[:, g * G + j, :])
            c = Chain(dve, ln_step)
            c.link(m)
            for t in range(NT):
                m = V.bn_aggr(mv[:, t, :], stats[:, t, :])
            c.link(m)
            veps, std, r, t1, t2, rstd = (small[:, i, :] for i in range(6))
            c.link(V.tensor_scalar(veps, mv[:, :, 1], EPS, None, ALU.add))
            assert c.n == NORM_VAR
            dve.wait_ge(std_ready, 1)
            c.link(V.reciprocal(r, std))
            c.link(V.tensor_tensor(t1, r, r, ALU.mult))
            c.link(V.tensor_tensor(t2, t1, veps, ALU.mult))
            c.link(V.tensor_scalar(t1, t2, -0.5, 1.5, ALU.mult, ALU.add))
            c.link(V.tensor_tensor(rstd, r, t1, ALU.mult))
            for t in range(NT):
                m = V.tensor_scalar(rec[:, t, ROW], acc[:, t, :], mv[:, t, 0:1], rstd[:, t:t + 1],
                                    ALU.subtract, ALU.mult)
                if t % G == G - 1:
                    m.then_inc(xn_ready, 1)

            c = Chain(dve, rt_step)

            def by_token(v):
                return v.unsqueeze(2).to_broadcast([P, NT, E])

            def by_expert(v):
                return v.unsqueeze(1).to_broadcast([P, NT, E])
            (m1, i1, m2, i2, ssum, e2, p1, p2, t1, t2, w1, w2, hi, lo) = (small[:, i, :] for i in range(14))
            dve.wait_ge(masks_ready, 1)
            dve.wait_ge(consts_in, 16 * N_CONST)
            dve.wait_ge(logits_mm, NG)
            c.link(V.tensor_tensor(L, PS[:, 4, 0:NT * E].rearrange("p (t e) -> p t e", e=E), by_expert(rbias[:, :]), ALU.add))
            c.link(V.tensor_reduce(m1, L, AX.X, ALU.max))
            V.tensor_tensor(ex, L, by_token(m1), ALU.subtract).then_inc(shifted, 1)

            def largest(values, m, i, mask):
                c.link(V.tensor_tensor(tmp, values, by_token(m), ALU.is_equal))
                c.link(V.scalar_tensor_tensor(tmp, tmp, -float(E), by_expert(expert_id_up[:, :]), ALU.mult, ALU.add))
                c.link(V.tensor_reduce(i, tmp, AX.X, ALU.min))
                c.link(V.tensor_tensor(mask, by_expert(expert_id[:, :]), by_token(i), ALU.is_equal))
            largest(L, m1, i1, first)
            c.link(V.scalar_tensor_tensor(L2, first, -3.0e38, L, ALU.mult, ALU.add))
            c.link(V.tensor_reduce(m2, L2, AX.X, ALU.max))
            V.tensor_tensor(e2, m2, m1, ALU.subtract).then_inc(shifted, 1)
            largest(L2, m2, i2, second)
            V.tensor_tensor(chosen, first, second, ALU.add).then_inc(chosen_ready, 1)
            dve.wait_ge(exp_ready, 2)
            c.link(V.tensor_reduce(ssum, ex, AX.X, ALU.add))
            c.link(V.reciprocal(p1, ssum))
            c.link(V.tensor_tensor(p2, e2, p1, ALU.mult))
            c.link(V.scalar_tensor_tensor(t1, p1, 1e-20, p2, ALU.add, ALU.add))
            c.link(V.reciprocal(t2, t1))
            c.link(V.tensor_tensor(w1, p1, t2, ALU.mult))
            c.link(V.tensor_tensor(w2, p2, t2, ALU.mult))
            c.link(V.tensor_tensor(t1, i1, i2, ALU.is_lt))
            c.link(V.tensor_tensor(t2, i1, i2, ALU.is_gt))
            c.link(V.tensor_tensor(p1, w1, t1, ALU.mult))
            c.link(V.tensor_tensor(p2, w2, t2, ALU.mult))
            c.link(V.tensor_tensor(rec[:, :, 1], p1, p2, ALU.add))
            c.link(V.tensor_tensor(p1, w1, t2, ALU.mult))
            c.link(V.tensor_tensor(p2, w2, t1, ALU.mult))
            c.link(V.tensor_tensor(rec[:, :, REC - 1], p1, p2, ALU.add))
            dve.wait_ge(counts_mm, 1)
            c.link(V.tensor_copy(totals, PS[:, 6, NT * E:2 * NT * E].rearrange("p (t e) -> p e t", e=E)))
            flat = "p e t -> p (e t)"
            c.link(V.tensor_tensor_scan(upto.rearrange(flat), same_expert[:, :, :].rearrange(flat),
                                        totals.rearrange(flat), 0.0, ALU.mult, ALU.add))
            n_tiles, ends, base = cols[:, 0, :], cols[:, 1, :], cols[:, 2, :]
            c.link(V.tensor_scalar(counts_i[:, 0, :], upto[:, :, NT - 1], float(P - 1), None, ALU.add))
            c.link(V.tensor_single_scalar(counts_i[:, 1, :], counts_i[:, 0, :], P.bit_length() - 1,
                                          ALU.logical_shift_right))
            c.link(V.tensor_copy(n_tiles, counts_i[:, 1, :]))
            c.link(V.tensor_tensor_scan(ends, ones[:, 0:E], n_tiles, 0.0, ALU.mult, ALU.add))
            c.link(V.tensor_tensor(base, ends, n_tiles, ALU.subtract))
            c.link(V.tensor_scalar(base, base, float(P), None, ALU.mult))
            c.link(V.tensor_tensor(upto, upto, totals, ALU.subtract))
            c.link(V.tensor_tensor(upto, upto, base.unsqueeze(2).to_broadcast([P, E, NT]), ALU.add))
            c.link(V.tensor_tensor(pos, PS[:, 6, 0:NT * E].rearrange("p (t e) -> p t e", e=E),
                                   upto.rearrange("p e t -> p t e"), ALU.add))
            c.link(V.tensor_tensor(pos, pos, chosen, ALU.mult))
            c.link(V.tensor_reduce(hi, pos, AX.X, ALU.max))
            c.link(V.tensor_reduce(lo, pos, AX.X, ALU.add))
            c.link(V.tensor_tensor(lo, lo, hi, ALU.subtract))
            V.tensor_scalar(slot_hi[:, :], hi, float(REC // 2), 1.0, ALU.mult, ALU.add)
            V.tensor_scalar(slot_lo[:, :], lo, float(REC // 2), None, ALU.mult).then_inc(routed, 1)
            dve.wait_ge(routed, 1)
            dve.wait_ge(bias_added, 1)
            num_psum = [PS[:, 4 + b, 0:2 * (D + HEADS)].rearrange("p (t w) -> p t w", t=2) for b in range(2)]
            seq = "p (b s) -> p b s"

            def attention_step(turn):
                if t := turn(1):
                    dve.wait_ge(loc_act, t.n + 1)
                    l3 = loc[:, t.k, :].rearrange(seq, s=S)
                    x3 = xT[:, bass.ds(t.n * GT, GT)].rearrange(seq, s=S)
                    V.scalar_tensor_tensor(l3[:, :, 1:S], x3[:, :, 0:S - 1], cw[:, 0:1], l3[:, :, 1:S],
                                           ALU.mult, ALU.add).then_inc(conv_step, 1)
                    dve.wait_ge(conv_step, t.n + 1)
                    V.scalar_tensor_tensor(l3[:, :, 0:S - 1], x3[:, :, 1:S], cw[:, 2:3], l3[:, :, 0:S - 1],
                                           ALU.mult, ALU.add).then_inc(loc_ready, 1)
                if t := turn(0):
                    dve.wait_ge(q_act, t.n + 1)
                    V.scalar_tensor_tensor(qT[:, t.k, :], PS[:, 0, :], 0.0, qT[:, t.k, :],
                                           ALU.max, ALU.add).then_inc(q_ready, 1)
                if t := turn(1):
                    dve.wait_ge(state_mm, t.n + 1)
                    if t.past(2):
                        dve.wait_ge(num_mm, t.n - 1)
                    st = PS[:, 3, 0:BG * (D + 1)].rearrange("p (b w) -> p b w", b=BG)
                    km = kvm[:, t.k * BG:(t.k + 1) * BG, :]
                    V.tensor_tensor(km[:, :, 0:D], st[:, :, 0:D], head_block[:, :, :].rearrange("p h d -> p (h d)")
                                    .unsqueeze(1).to_broadcast([P, BG, D]), ALU.mult)
                    V.tensor_tensor(km[:, :, D:D + HEADS], st[:, :, D:D + 1].to_broadcast([P, BG, HEADS]),
                                    head_rows[:, :].unsqueeze(1).to_broadcast([P, BG, HEADS]), ALU.mult).then_inc(kvm_ready, 1)
                if t := turn(2):
                    dve.wait_ge(atT_mm, t.n + 1)
                    dve.wait_ge(loc_ready, t.n + 1)
                    if t.past(2):
                        dve.wait_ge(proj_mm, t.n - 1)
                    V.tensor_tensor(atT[:, t.k, :], PS[:, 6, :], loc[:, t.k, :], ALU.add).then_inc(at_ready, 1)
                if t := turn(0):
                    dve.wait_ge(k_act, t.n + 1)
                    kk = kb[:, t.k * G:(t.k + 1) * G, :]
                    V.scalar_tensor_tensor(kk, kv_psum[:, :, 0:D], 0.0, kk, ALU.max, ALU.add).then_inc(k_ready, 1)
                if t := turn(1):
                    dve.wait_ge(num_mm, t.n + 1)
                    for b in range(2):
                        m = V.tensor_scalar(den[:, 2 * b:2 * b + 2, :], num_psum[b][:, :, D:D + HEADS], 1e-6, None, ALU.max)
                    m.then_inc(num_step, 1)
                    dve.wait_ge(num_step, 2 * t.n + 1)
                    V.reciprocal(rden, den).then_inc(num_step, 1)
                    dve.wait_ge(num_step, 2 * t.n + 2)
                    if t.past(1):
                        dve.wait_ge(atT_mm, t.n)
                    for b in range(2):
                        m = V.tensor_tensor(attn[:, 2 * b:2 * b + 2, :].rearrange("p t (h d) -> p t h d", d=HD),
                                            num_psum[b][:, :, 0:D].rearrange("p t (h d) -> p t h d", d=HD),
                                            rden[:, 2 * b:2 * b + 2, :].unsqueeze(3).to_broadcast([P, 2, HEADS, HD]),
                                            ALU.mult)
                    m.then_inc(attn_ready, 1)
                if t := turn(2):
                    dve.wait_ge(proj_mm, t.n + 1)
                    a = acc[:, bass.ds(t.n * G, G), :].rearrange("p t d -> p (t d)")
                    V.tensor_tensor(a, PS[:, 7, :], a, ALU.add).then_inc(proj_added, 1)
            pipeline(dve, NG, 2, 2, attention_step, peeled=2)

            c = Chain(dve, tile_step)
            at, nxt = tile_ends[:, 0, :], tile_ends[:, 1, :]
            c.link(V.tensor_scalar(at, tile_no[:, :], ends[:, 0:1], None, ALU.is_ge))
            for e in range(1, E - 1):
                c.link(V.scalar_tensor_tensor(nxt, tile_no[:, :], ends[:, e:e + 1], at, ALU.is_ge, ALU.add))
                at, nxt = nxt, at
            V.tensor_copy(tile_expert[:, :], at).then_inc(tiles_ready, 1)

            def shared_step(turn):
                if t := turn(3):
                    dve.wait_ge(sh_y_act, t.n + 1)
                    a = acc[:, bass.ds(t.n * G, G), :]
                    V.tensor_tensor(a, PS[:, 4 + 2 * t.k:6 + 2 * t.k, :].rearrange("p b (t w) -> p (b t) w", w=2 * P)[:, :, 0:P],
                                    a, ALU.add).then_inc(sh_step, 1)
                    dve.wait_ge(sh_step, t.n + 1)
                    V.tensor_tensor(a, a, y_s, ALU.add).then_inc(sh_added, 1)
                gu, before_gu = turn(1), turn(2)
                for c in range(NC):
                    if gu:
                        par, m, f = (gu.k + c) % 2, gu.n * NC + c, FC[c]
                        dve.wait_ge(sh_silu, m + 1)
                        if gu.past(1) or c >= 2:
                            dve.wait_ge(sh_hl, m - 1)
                        V.tensor_tensor(h_s[0:f, par, :], PS[0:f, 2 + par, :], silu_s[0:f, par, :], ALU.mult).then_inc(sh_h, 1)
                    t, c1 = (gu, c - 1) if c else (before_gu, NC - 1)
                    if t:
                        dve.wait_ge(sh_hh, t.n * NC + c1 + 1)
                        V.tensor_tensor(hl_s[0:FC[c1], t.k * NC + c1, :], h_s[0:FC[c1], (t.k + c1) % 2, :],
                                        hh_s[0:FC[c1], t.k * NC + c1, :].bitcast(F32), ALU.subtract).then_inc(sh_hl, 1)
                    if c == 0 and (t := turn(0)):
                        dve.wait_ge(sh_xh, t.n + 1)
                        V.tensor_tensor(xl_s[:, t.k, :], xT[:, bass.ds(t.n * GT, GT)], xh_s[:, t.k, :].bitcast(F32),
                                        ALU.subtract).then_inc(sh_xl, 1)
            pipeline(dve, NG, 3, 2, shared_step, peeled=2)

            dve.wait_ge(sh_added, NG)
            V.memset(h_e[:, :, F:FP], 0.0).then_inc(h_clear, 1)
            def expert_step(turn):
                if t := turn(0):
                    dve.wait_ge(ex_xh, t.n + 1)
                    p = t.k % 2
                    V.tensor_tensor(xl_e[:, p, :], PS[:, 6, 0:P], xh_e[:, p, :].bitcast(F32),
                                    ALU.subtract).then_inc(ex_xl, 1)
                if t := turn(1):
                    p = t.k % 2
                    dve.wait_ge(ex_silu, t.n + 1)
                    if t.past(2):
                        dve.wait_ge(ex_hT_mm, t.n - 1)
                    V.tensor_tensor(h_e[:, p, 0:F], PS[:, 2 + p, 0:F], silu_e[:, p, :], ALU.mult).then_inc(ex_h, 1)
                if t := turn(2):
                    p = t.k % 2
                    dve.wait_ge(ex_hh, t.n + 1)
                    V.tensor_tensor(hl_e[:, p, :], PS[:, 4 + p, 0:FP], hh_e[:, p, :].bitcast(F32),
                                    ALU.subtract).then_inc(ex_hl, 1)
                if t := turn(3):
                    p = t.k % 2
                    dve.wait_ge(ex_y_act, t.n + 1)
                    if t.past(4):
                        dve.wait_ge(y_sent[t.k % 4], 16 * (2 * t.r + t.k // 4))
                    V.scalar_tensor_tensor(y_buf[:, t.k % 4, :], PS[:, 7, 0:P],
                                           wslot[:, t.k:t.k + 1], y_half[:, p, :], ALU.mult, ALU.add).then_inc(ex_y, 1)
            pipeline(dve, TILES, 3, 8, expert_step)

            Q = NT // 4
            for j in range(4):
                dve.wait_ge(pair_in[j], 32)
                a = acc[:, j * Q:(j + 1) * Q, :]
                V.tensor_tensor(a, a, xT[:, j * Q * P:(j + 1) * Q * P].rearrange("p (t d) -> p t d", d=D),
                                ALU.add).then_inc(fin_step, 1)
                dve.wait_ge(fin_step, j + 1)
                V.tensor_tensor(a, a, rec[:, j * Q:(j + 1) * Q, ROW], ALU.add).then_inc(fin_ready, 1)


_SHAPES = [("L0_attn_bp", None), ("L0_attn_conv_w", None), ("L0_attn_conv_b", None), ("L0_ffn_router_w", None),
           ("L0_ffn_router_b", None), ("L0_ffn_gate_w", None), ("L0_ffn_up_w", None), ("L0_ffn_down_w", None),
           ("L0_ffn_sh_gate_w", None), ("L0_ffn_sh_up_w", None), ("L0_ffn_sh_down_w", None)]


def kernel(**inputs):
    import concourse.bacc as bacc
    from concourse.bass_utils import run_bass_kernel_spmd

    nc = bacc.Bacc("TRN2", target_bir_lowering=False, num_devices=1)
    arrays = {}

    def dram(name, a):
        a = np.ascontiguousarray(a)
        arrays[name] = a
        return nc.dram_tensor(name, a.shape, mybir.dt.from_np(a.dtype), kind="ExternalInput").ap()

    x = dram("x", inputs["L0_attn_x"])
    wqT = dram("wqT", np.asarray(inputs["L0_attn_Wq"]).T)
    wkvT = dram("wkvT", np.concatenate([np.asarray(inputs["L0_attn_Wk"]).T, np.asarray(inputs["L0_attn_Wv"]).T], axis=1))
    wpT = dram("wpT", np.asarray(inputs["L0_attn_Wp"]).T)
    rest = [dram(name, inputs[name]) for name, _ in _SHAPES]
    out = nc.dram_tensor("out", x.shape, F32, kind="ExternalOutput").ap()
    tokens, d = x.shape[0] * x.shape[1], x.shape[2]
    n_slots = (2 * tokens // P + inputs["L0_ffn_gate_w"].shape[0]) * P
    slots = nc.dram_tensor("slots", (n_slots, d + 4), F32, kind="Internal").ap()
    pair_out = nc.dram_tensor("pair_out", (2 * tokens + n_slots, d), F32, kind="Internal").ap()
    build(nc, x, wqT, wkvT, wpT, *rest, out, slots, pair_out)
    got = run_bass_kernel_spmd(nc, [arrays], core_ids=[0])
    return got.results[0]["out"]
```
